# Optimizing a Trainium2 kernel written in Bass

```python
import numpy as np
import jax
import jax.numpy as jnp

def _softmax(x, axis=-1):
    return jax.nn.softmax(x, axis=axis)

def _gelu(x):
    return jax.nn.gelu(x, approximate=True)

def _silu(x):
    return jax.nn.silu(x)

def _sigmoid(x):
    return jax.nn.sigmoid(x)

def _layernorm(x, axis=-1, eps=1e-05):
    m = jnp.mean(x, axis=axis, keepdims=True)
    v = jnp.var(x, axis=axis, keepdims=True)
    return (x - m) / jnp.sqrt(v + eps)

def _scatter_add(tgt, idx, src, axis=0):
    return tgt.at[idx].add(src)

def _segment_sum(src, seg, n):
    return jax.ops.segment_sum(src, seg, n)
kernel_name = 'mk_gnn_preln_d1_gnn_r8_d5002e'

def setup_inputs(seed: int=0):
    np.random.seed(seed)
    _w = jnp.asarray

    def _rec_inputs():
        import jax
        import jax.numpy as jnp
        _gk = jax.random.key(seed)
        x = -0.0003713 + 1 * jax.random.normal(jax.random.fold_in(_gk, 1), (6250, 256), jnp.float32)
        src = jax.random.randint(jax.random.fold_in(_gk, 2), (200000,), 0, 6250, jnp.int32)
        dst = jnp.minimum((6250 * jax.random.uniform(jax.random.fold_in(_gk, 3), (200000,)) ** 2.0).astype(jnp.int32), 49999)
        _o = jnp.argsort(dst, stable=True)
        src = src[_o]
        dst = dst[_o]
        edge_weight1 = -0.00278149 + 0.998712 * jax.random.normal(jax.random.fold_in(_gk, 12), (200000, 1), jnp.float32)
        return (x, src, dst, edge_weight1)
    x, src, dst, edge_weight1 = _rec_inputs()

    def _L0_gnn_setup():
        import jax, jax.numpy as jnp
        import numpy as np
        N_NODES = 6250
        N_EDGES = 40000
        HID = 256
        EDIM = 1
        NUM_LAYERS = 2

        def _init_linear(key, fan_in, fan_out):
            kw, kb = jax.random.split(key)
            bound = 1.0 / np.sqrt(fan_in)
            W = jax.random.uniform(kw, (fan_in, fan_out), jnp.float32, -bound, bound)
            b = jax.random.uniform(kb, (fan_out,), jnp.float32, -bound, bound)
            return (W, b)

        def _layer(x, edge_index, edge_attr, eW1, eb1, eW2, eb2, nW1, nb1, nW2, nb2):
            idx_i, idx_j = (edge_index[0], edge_index[1])
            e = jax.nn.relu(edge_attr @ eW1 + eb1) @ eW2 + eb2
            msg = e + x[idx_j]
            agg = jax.ops.segment_sum(msg, idx_i, num_segments=N_NODES)
            h = jnp.concatenate([x, agg], axis=-1)
            return jax.nn.relu(h @ nW1 + nb1) @ nW2 + nb2
        key = jax.random.key(seed)
        ks = jax.random.split(key, 3 + 4 * NUM_LAYERS)
        inp = {'z': jax.random.normal(ks[0], (N_NODES, HID), jnp.float32), 'edge_index': jax.random.randint(ks[1], (2, N_EDGES), 0, N_NODES, jnp.int64 if jax.config.jax_enable_x64 else jnp.int32), 'edge_attr': jax.random.normal(ks[2], (N_EDGES, EDIM), jnp.float32)}
        k = 3
        for l in range(NUM_LAYERS):
            eW1, eb1 = _init_linear(ks[k + 0], EDIM, HID)
            eW2, eb2 = _init_linear(ks[k + 1], HID, HID)
            nW1, nb1 = _init_linear(ks[k + 2], 2 * HID, HID)
            nW2, nb2 = _init_linear(ks[k + 3], HID, HID)
            inp[f'l{l}_eW1'], inp[f'l{l}_eb1'] = (eW1, eb1)
            inp[f'l{l}_eW2'], inp[f'l{l}_eb2'] = (eW2, eb2)
            inp[f'l{l}_nW1'], inp[f'l{l}_nb1'] = (nW1, nb1)
            inp[f'l{l}_nW2'], inp[f'l{l}_nb2'] = (nW2, nb2)
            k += 4
        return inp
    _L0_gnn_all = _L0_gnn_setup()
    _L0_gnn_in = {k: v for k, v in _L0_gnn_all.items() if k in ('l0_eW1', 'l0_eb1', 'l0_eW2', 'l0_eb2', 'l0_nW1', 'l0_nb1', 'l0_nW2', 'l0_nb2', 'l1_eW1', 'l1_eb1', 'l1_eW2', 'l1_eb2', 'l1_nW1', 'l1_nb1', 'l1_nW2', 'l1_nb2')}
    del _L0_gnn_all
    return {'x': x, 'src': src, 'dst': dst, 'edge_weight1': edge_weight1, 'L0_gnn_l0_eW1': _L0_gnn_in['l0_eW1'], 'L0_gnn_l0_eb1': _L0_gnn_in['l0_eb1'], 'L0_gnn_l0_eW2': _L0_gnn_in['l0_eW2'], 'L0_gnn_l0_eb2': _L0_gnn_in['l0_eb2'], 'L0_gnn_l0_nW1': _L0_gnn_in['l0_nW1'], 'L0_gnn_l0_nb1': _L0_gnn_in['l0_nb1'], 'L0_gnn_l0_nW2': _L0_gnn_in['l0_nW2'], 'L0_gnn_l0_nb2': _L0_gnn_in['l0_nb2'], 'L0_gnn_l1_eW1': _L0_gnn_in['l1_eW1'], 'L0_gnn_l1_eb1': _L0_gnn_in['l1_eb1'], 'L0_gnn_l1_eW2': _L0_gnn_in['l1_eW2'], 'L0_gnn_l1_eb2': _L0_gnn_in['l1_eb2'], 'L0_gnn_l1_nW1': _L0_gnn_in['l1_nW1'], 'L0_gnn_l1_nb1': _L0_gnn_in['l1_nb1'], 'L0_gnn_l1_nW2': _L0_gnn_in['l1_nW2'], 'L0_gnn_l1_nb2': _L0_gnn_in['l1_nb2']}

def reference(x, src, dst, edge_weight1, L0_gnn_l0_eW1, L0_gnn_l0_eb1, L0_gnn_l0_eW2, L0_gnn_l0_eb2, L0_gnn_l0_nW1, L0_gnn_l0_nb1, L0_gnn_l0_nW2, L0_gnn_l0_nb2, L0_gnn_l1_eW1, L0_gnn_l1_eb1, L0_gnn_l1_eW2, L0_gnn_l1_eb2, L0_gnn_l1_nW1, L0_gnn_l1_nb1, L0_gnn_l1_nW2, L0_gnn_l1_nb2):
    import jax
    import jax.numpy as jnp

    def _L0_gnn_ref(z, edge_index, edge_attr, l0_eW1, l0_eb1, l0_eW2, l0_eb2, l0_nW1, l0_nb1, l0_nW2, l0_nb2, l1_eW1, l1_eb1, l1_eW2, l1_eb2, l1_nW1, l1_nb1, l1_nW2, l1_nb2):
        import jax, jax.numpy as jnp
        import numpy as np
        N_NODES = 6250
        N_EDGES = 40000
        HID = 256
        EDIM = 1
        NUM_LAYERS = 2

        def _init_linear(key, fan_in, fan_out):
            kw, kb = jax.random.split(key)
            bound = 1.0 / np.sqrt(fan_in)
            W = jax.random.uniform(kw, (fan_in, fan_out), jnp.float32, -bound, bound)
            b = jax.random.uniform(kb, (fan_out,), jnp.float32, -bound, bound)
            return (W, b)

        def _layer(x, edge_index, edge_attr, eW1, eb1, eW2, eb2, nW1, nb1, nW2, nb2):
            idx_i, idx_j = (edge_index[0], edge_index[1])
            e = jax.nn.relu(edge_attr @ eW1 + eb1) @ eW2 + eb2
            msg = e + x[idx_j]
            agg = jax.ops.segment_sum(msg, idx_i, num_segments=N_NODES)
            h = jnp.concatenate([x, agg], axis=-1)
            return jax.nn.relu(h @ nW1 + nb1) @ nW2 + nb2
        layer_params = [(l0_eW1, l0_eb1, l0_eW2, l0_eb2, l0_nW1, l0_nb1, l0_nW2, l0_nb2), (l1_eW1, l1_eb1, l1_eW2, l1_eb2, l1_nW1, l1_nb1, l1_nW2, l1_nb2)]
        out = z
        for p in layer_params:
            out = out + _layer(out, edge_index, edge_attr, *p)
        return out
    edge_index = jnp.stack([src, dst])
    h = jnp.maximum(_layernorm(x, axis=-1), 0.0)
    x = x + _L0_gnn_ref(h, edge_index, edge_weight1, L0_gnn_l0_eW1, L0_gnn_l0_eb1, L0_gnn_l0_eW2, L0_gnn_l0_eb2, L0_gnn_l0_nW1, L0_gnn_l0_nb1, L0_gnn_l0_nW2, L0_gnn_l0_nb2, L0_gnn_l1_eW1, L0_gnn_l1_eb1, L0_gnn_l1_eW2, L0_gnn_l1_eb2, L0_gnn_l1_nW1, L0_gnn_l1_nb1, L0_gnn_l1_nW2, L0_gnn_l1_nb2)
    return x

_drawn_inputs = setup_inputs


def setup_inputs(seed=0):
    import zlib

    import numpy as np

    out = dict(_drawn_inputs(seed))
    spreads = {}
    factors = {'L0_gnn_l0_nb1': 8.0,
     'L0_gnn_l0_nb2': 4.204,
     'L0_gnn_l1_eb2': 4.107,
     'L0_gnn_l1_nb1': 64.0,
     'L0_gnn_l1_nb2': 8.0}
    for name, (base, spread) in spreads.items():
        noise = np.random.default_rng([zlib.crc32(name.encode()), seed]).standard_normal(out[name].shape)
        drawn = base * np.exp(spread * noise) if base else spread * noise
        out[name] = jnp.asarray(drawn.astype(out[name].dtype))
    for name, factor in factors.items():
        out[name] = (out[name] * factor).astype(out[name].dtype)
    return out
```

```python
from contextlib import ExitStack

import concourse.bass as bass
from concourse import mybir

F32 = mybir.dt.float32
BF16 = mybir.dt.bfloat16
I32 = mybir.dt.int32
U32 = mybir.dt.uint32
U16 = mybir.dt.uint16
ALU = mybir.AluOpType
ACT = mybir.ActivationFunctionType
AXX = mybir.AxisListType.X

P = 128
N_NODES = 6250
N_EDGES = 200000
H = 256
HC = H // P
LAYERS = 2
EPS = 1e-5
TINY = 1e-30

BLOCKS = -(-N_NODES // P)
BUCKETS = BLOCKS + 1
GROUP = 2 * P
GROUPS = -(-(N_EDGES // GROUP + BLOCKS) // 4) * 4
TILES = 2 * GROUPS
PASSES = GROUPS // 4

STEP = 8
ECOLS = -(-N_EDGES // (P * 4 * STEP)) * 4 * STEP
STEPS = ECOLS // STEP
ROUNDS = STEPS // 4
FULL_P = N_EDGES // ECOLS
LAST_C = N_EDGES - FULL_P * ECOLS
TCOLS = TILES + -(-(P * ECOLS - N_EDGES) // P)
FILL_REPS = 10
FILL_COLS = TCOLS // FILL_REPS
KEY = 256
NO_NODE = P
LN_ROWS = 125
LN_TILES = N_NODES // LN_ROWS
LAST_ROWS = N_NODES - (BLOCKS - 1) * P

XCOL = HC * 2 * P
DCOL = XCOL + HC * P
BCOLS = DCOL + 4
OPS = 14


def ge(eng, sem, value):
    if not (isinstance(value, int) and value <= 0):
        eng.wait_ge(sem, value)


def hold(eng):
    eng.nop(nofuse=True)


def over_blocks(eng, step):
    step(-1, 1, 0, True, False, False)
    step(0, 0, 0, True, True, False)
    step(1, 1, 1, True, True, True)
    step(2, 0, 1, True, True, True)
    with eng.Fori(0, (BLOCKS - 5) // 2) as pair:
        step(2 * pair + 3, 1, pair + 2, True, True, True)
        step(2 * pair + 4, 0, pair + 2, True, True, True)
    step(BLOCKS - 2, 1, (BLOCKS - 1) // 2, True, True, True)
    step(BLOCKS - 1, 0, (BLOCKS - 1) // 2, False, True, True)
    step(BLOCKS, 1, (BLOCKS + 1) // 2, False, False, True)


def gnn(nc, x, src, dst, ew, eW1, eb1, eW2, eb2, nW1, nb1, nW2, nb2, out):
    table = nc.dram_tensor("sorted_edges", [P * TCOLS, 2], F32, kind="Internal").ap()
    z_rows = nc.dram_tensor("z_rows", [BLOCKS * P, H], F32, kind="Internal").ap()
    split_rows = [nc.dram_tensor(f"split_rows{l}", [rows, 3 * H], BF16, kind="Internal").ap()
                  for l, rows in enumerate((N_NODES, BLOCKS * P))]
    with ExitStack() as ctx:
        def sb(name, shape, dt):
            return ctx.enter_context(nc.sbuf_tensor(name, shape, dt))

        def sem(name):
            return ctx.enter_context(nc.semaphore(name))

        sums = sb("sums", [P, BLOCKS * BCOLS], F32)
        dst_all = sb("dst_all", [P, TILES], U16)
        a_all = sb("a_all", [P, TILES], F32)
        parts = sb("parts", [P, TILES, 4], BF16)
        local = sb("local", [P, TILES], BF16)
        work = sb("work", [P, 4608], F32)
        thresh = sb("thresh", [P, H], F32)
        wx = sb("wx", [P, HC, H], F32)
        wa = sb("wa", [P, HC, H], F32)
        we = sb("we", [P, HC, H], F32)
        w2 = sb("w2", [P, HC, H], F32)
        wd = sb("wd", [4, H], F32)
        nb2_row = sb("nb2_row", [P, H], F32)
        w_col = sb("w_col", [P, HC], F32)
        b_col = sb("b_col", [P, HC], F32)
        eb2_col = sb("eb2_col", [P, HC], F32)
        nb1_col = sb("nb1_col", [P, HC], F32)
        s_col = sb("s_col", [P, HC], F32)
        wh_col = sb("wh_col", [P, HC], F32)
        bh_col = sb("bh_col", [P, HC], F32)
        iota_b = sb("iota_b", [P, P], BF16)
        ident = sb("ident", [P, P], F32)
        d_in = sb("d_in", [P, 2, 4], F32)
        zero_col = sb("zero_col", [P, 1], F32)
        eps_col = sb("eps_col", [P, 1], F32)
        group_block = sb("group_block", [1, GROUPS], I32)
        idx_now = sb("idx_now", [P, 4, 2], U32)

        gath = work[:, 0:3072].bitcast(BF16).rearrange("p (g j n) -> p g j n", g=4, j=2)
        hots = work[:, 3072:4096].bitcast(BF16).rearrange("p (g j n) -> p g j n", g=2, j=2)
        signs = work[:, 4096:4608].bitcast(BF16).rearrange("p (g j n) -> p g j n", g=2, j=2)
        ew2_in = work[:, 0:512].rearrange("p (c n) -> p c n", c=HC)
        ew2_T = work[:, 512:1024].rearrange("p (c n) -> p c n", c=HC)
        d_cols = work[:, 1024:1040].rearrange("p (c n) -> p c n", c=4)
        w_row, b_row, s_row, m_row = (work[:, 3072 + H * k:3072 + H * k + H] for k in range(4))

        def two(start, n):
            return [work[:, start:start + n], work[:, start + n:start + 2 * n]]

        z_in, z_T, rel, hid, z_bias, z_out = (two(2 * H * k, H) for k in range(6))
        z_split = [v.bitcast(BF16) for v in two(3072, 3 * H // 2)]
        x_in = two(3072, H)
        residue = work[:, 3840:4096]
        scaled = work[:, 4096:4352]
        d_T = [work[0:4, 4352:4480], work[0:4, 4480:4608]]

        taken = [0]

        def early(n, dt=F32):
            v = sums[:, taken[0]:taken[0] + n]
            taken[0] += n
            return v if dt == F32 else v.bitcast(dt)

        src_i = early(ECOLS, I32)
        dst_i = early(ECOLS, I32)
        a_e = early(ECOLS)
        blk_i = early(ECOLS, I32)
        blk_f = early(ECOLS)
        key_f = early(ECOLS)
        blk_b = early(ECOLS // 2, BF16)
        same = [early(ECOLS // 2, BF16) for _ in range(2)]
        fill = early(2 * FILL_COLS).rearrange("p (c w) -> p c w", w=2)
        iota_i = early(GROUPS, I32)
        iota_f = early(GROUPS)
        started = early(GROUPS)
        later = early(P)
        ones = early(P)
        counts = early(BUCKETS)
        quot_f = early(1)
        quot_i = early(2, I32)
        quot_rows = early(P)
        run = early(STEP * BUCKETS).rearrange("p (j b) -> p j b", j=STEP)
        hot = early(STEP * BUCKETS).rearrange("p (j b) -> p j b", j=STEP)
        prod = early(STEP * BUCKETS).rearrange("p (j b) -> p j b", j=STEP)
        pos_f = early(STEP)
        pos_i = early(STEP, I32)
        pos_p = early(STEP, I32)
        pos_c = early(STEP, I32)
        row_now = early(2 * STEP, U32).rearrange("p (h j) -> p h j", h=2)
        rec_now = early(4 * STEP).rearrange("p (h j w) -> p h j w", h=2, w=2)
        ln_x = early(H)
        ln_y = early(H)
        ln_z = early(H)
        ln_r = early(H)
        ln_split = early(3 * H // 2, BF16)
        ln_stats = early(6)
        ln_mv = early(2)
        ln_std = early(1)
        ln_rstd = early(1)
        early_end = taken[0]
        tab = sums[:, 0:2 * TILES].rearrange("p (t w) -> p t w", w=2)
        key_i = sums[:, 2 * TILES:3 * TILES].bitcast(I32)
        dst_part = sums[:, 3 * TILES:4 * TILES].bitcast(I32)
        node_part = sums[:, 4 * TILES:5 * TILES].bitcast(I32)
        a_rest = sums[:, 5 * TILES:6 * TILES]
        assert 6 * TILES <= early_end

        def block_sums(b, start, n):
            return sums[:, bass.ds(b * BCOLS + start, n)]

        ps = [ctx.enter_context(nc.psum_tensor(f"ps{i}", [P, 1024], F32)) for i in range(2)]
        ps_d = [ctx.enter_context(nc.psum_tensor(f"ps_d{i}", [P, 512], F32)) for i in range(2)]
        ps_out = [ctx.enter_context(nc.psum_tensor(f"ps_out{i}", [P, 512], F32)) for i in range(2)]

        pads_set, src_in, edges_in, table_filled, consts, consts_v = map(
            sem, "pads_set src_in edges_in table_filled consts consts_v".split())
        keyed, counted, totals, quot, bases, ran, starts, grouped, blocks_known = map(
            sem, "keyed counted totals quot bases ran starts grouped blocks_known".split())
        ranked, rows_ready, recs_ready, table_in = map(
            sem, "ranked rows_ready recs_ready table_in".split())
        scattered = [sem("scattered0"), sem("scattered1")]
        ln_in, ln_vec, ln_act, ln_out = map(sem, "ln_in ln_vec ln_act ln_out".split())
        unpacked_v, unpacked_a, cleared = map(sem, "unpacked_v unpacked_a cleared".split())
        weights_in, prep_v, ew2_turned, ew2_kept, we_summed, we_kept, wd_summed, prepared = map(
            sem, "weights_in prep_v ew2_turned ew2_kept we_summed we_kept wd_summed prepared".split())
        staged, hots_ready, signs_ready, group_done, added = map(
            sem, "staged hots_ready signs_ready group_done added".split())
        landed = [sem(f"landed{g}") for g in range(4)]
        turned, zT_ready, dT_ready, rel_ready, hid_summed, hid_ready, out_summed = map(
            sem, "turned zT_ready dT_ready rel_ready hid_summed hid_ready out_summed".split())
        d_taken, bias_added, z_ready, hi_ready, res_ready, mid_ready, lo_ready = map(
            sem, "d_taken bias_added z_ready hi_ready res_ready mid_ready lo_ready".split())
        x_added, emptied = sem("x_added"), sem("emptied")
        z_loaded, x_loaded, stored = ([sem(f"{n}{i}") for i in range(2)] for n in ("z_loaded", "x_loaded", "stored"))
        fills = [(BLOCKS + 1) // 2, BLOCKS // 2]

        block = ctx.enter_context(nc.Block())
        W_DMAS = 11

        def flat(v):
            return v.rearrange("a n -> (a n)")

        def everywhere(v):
            return v.rearrange("(a n) -> a n", a=1).broadcast_to([P, H])

        @block.sync
        def _(sp):
            def edges(dest, v, done):
                sp.dma_start(dest[0:FULL_P, :], v[0:FULL_P * ECOLS].rearrange("(p c) -> p c", c=ECOLS)
                             ).then_inc(done, 16)
                sp.dma_start(dest[FULL_P:FULL_P + 1, 0:LAST_C],
                             v[FULL_P * ECOLS:N_EDGES].rearrange("(p c) -> p c", p=1)).then_inc(done, 16)

            sp.wait_ge(pads_set, 4)
            edges(src_i, src, src_in)
            edges(dst_i, dst, edges_in)
            edges(a_e, ew.rearrange("e w -> (e w)"), edges_in)
            sp.dma_start(table.rearrange("(p r n) w -> p r (n w)", p=P, r=FILL_REPS),
                         fill[:, :, :].rearrange("p (r c) w -> p r (c w)", r=1)
                         .broadcast_to([P, FILL_REPS, 2 * FILL_COLS])).then_inc(table_filled, 16)
            sp.dma_start(z_rows[N_NODES:BLOCKS * P, :], ln_z[0:BLOCKS * P - N_NODES, :]
                         ).then_inc(table_filled, 16)

            def layernorm(t):
                ge(sp, ln_vec, 6 * t)
                sp.dma_start(ln_x[0:LN_ROWS, :], x[bass.ds(t * LN_ROWS, LN_ROWS), :]).then_inc(ln_in, 16)
                sp.wait_ge(ln_vec, 6 * t + 6)
                sp.dma_start(z_rows[bass.ds(t * LN_ROWS, LN_ROWS), :], ln_z[0:LN_ROWS, :]
                             ).then_inc(ln_out, 16)
                sp.dma_start(split_rows[0][bass.ds(t * LN_ROWS, LN_ROWS), :], ln_split[0:LN_ROWS, :]
                             ).then_inc(ln_out, 16)

            def weights(l):
                for dest, v in ((w_row, flat(eW1[l])), (b_row, eb1[l]), (nb2_row[:, :], nb2[l])):
                    sp.dma_start(dest, everywhere(v)).then_inc(weights_in, 16)
                for dest, v in ((w_col, flat(eW1[l])), (b_col, eb1[l]), (eb2_col, eb2[l]), (nb1_col, nb1[l])):
                    sp.dma_start(dest[:, :], v.rearrange("(c p) -> p c", p=P),
                                 allow_slow_non_contiguous=True).then_inc(weights_in, 16)
                for dest, v in ((wx, nW1[l][0:H, :]), (wa, nW1[l][H:2 * H, :]), (w2, nW2[l]), (ew2_in, eW2[l])):
                    sp.dma_start(dest[:, :, :], v.rearrange("(c p) n -> p c n", p=P)).then_inc(weights_in, 16)

            weights(0)
            sp.wait_ge(table_filled, 32)
            layernorm(0)
            with sp.Fori(1, LN_TILES) as t:
                layernorm(t)
            for h in range(2):
                sp.wait_ge(scattered[h], STEPS // 2 * STEP * 16)
            sp.dma_start(tab, table.rearrange("(p t) w -> p t w", p=P)[:, 0:TILES, :]).then_inc(table_in, 16)

            for l in range(LAYERS):
                first = l * BLOCKS
                last = l == LAYERS - 1
                sp.wait_ge(added, (l + 1) * GROUPS)

                def mlp_io(b, i, turn, lead, main, trail):
                    if lead:
                        ge(sp, bias_added, first + b)
                        ge(sp, turned, first + b)
                        sp.dma_start(z_in[1 - i], z_rows[bass.ds((b + 1) * P, P), :]).then_inc(z_loaded[1 - i], 16)
                        if last:
                            ge(sp, x_added, b)
                            if isinstance(b, int) and b + 1 == BLOCKS - 1:
                                sp.dma_start(x_in[1 - i][0:LAST_ROWS, :], x[(b + 1) * P:N_NODES, :]
                                             ).then_inc(x_loaded[1 - i], 16)
                            else:
                                sp.dma_start(x_in[1 - i], x[bass.ds((b + 1) * P, P), :]).then_inc(x_loaded[1 - i], 16)
                    if trail:
                        if last:
                            ge(sp, z_ready, first + b)
                            if isinstance(b, int) and b == BLOCKS:
                                sp.dma_start(out[(b - 1) * P:N_NODES, :], z_out[1 - i][0:LAST_ROWS, :]
                                             ).then_inc(stored[1 - i], 16)
                            else:
                                sp.dma_start(out[bass.ds((b - 1) * P, P), :], z_out[1 - i]).then_inc(stored[1 - i], 16)
                        else:
                            ge(sp, lo_ready, b)
                            sp.dma_start(z_rows[bass.ds((b - 1) * P, P), :], z_out[1 - i]).then_inc(stored[1 - i], 16)
                            sp.dma_start(split_rows[l + 1][bass.ds((b - 1) * P, P), :], z_split[1 - i]
                                         ).then_inc(stored[1 - i], 16)

                over_blocks(sp, mlp_io)
                for i in range(2):
                    sp.wait_ge(stored[i], fills[i] * (32 * l + (16 if last else 32)))
                if not last:
                    weights(l + 1)

        @block.gpsimd
        def _(pool):
            tail = slice(P // 4 * 3, P)
            pool.memset(src_i[tail, LAST_C:ECOLS], BLOCKS * P).then_inc(pads_set, 1)
            pool.memset(dst_i[tail, LAST_C:ECOLS], 0).then_inc(pads_set, 1)
            pool.memset(a_e[tail, LAST_C:ECOLS], 0.0).then_inc(pads_set, 1)
            pool.wait_ge(pads_set, 3)
            pool.memset(fill[:, :, 0:1], float(NO_NODE)).then_inc(consts, 1)
            pool.memset(fill[:, :, 1:2], 0.0).then_inc(consts, 1)
            pool.memset(ln_z[:, :], 0.0).then_inc(consts, 1)
            pool.memset(ones[:, :], 1.0).then_inc(consts, 1)
            pool.memset(zero_col[:, :], 0.0).then_inc(consts, 1)
            pool.memset(eps_col[:, :], EPS).then_inc(consts, 1)
            pool.iota(iota_i[:, :], pattern=[[1, GROUPS]], base=0, channel_multiplier=0).then_inc(consts, 1)
            pool.wait_ge(consts, 7)
            pool.sem_inc(pads_set, 1)
            pool.affine_select(out=later[:, :], in_=ones[:, :], compare_op=ALU.is_gt, fill=0.0, base=0,
                               pattern=[[1, P]], channel_multiplier=-1).then_inc(consts, 1)
            pool.affine_select(out=ident[:, :], in_=ones[:, :], compare_op=ALU.is_equal, fill=0.0, base=0,
                               pattern=[[1, P]], channel_multiplier=-1).then_inc(consts, 1)
            pool.memset(parts[:, :, 0:1], 1.0).then_inc(consts, 1)
            pool.memset(sums[:, early_end:BLOCKS * BCOLS], 0.0).then_inc(cleared, 1)
            pool.wait_ge(table_filled, 32)

            def scatter(s, h):
                pool.wait_ge(rows_ready, s + 1)
                pool.wait_ge(recs_ready, s + 1)
                hold(pool)
                for j in range(STEP):
                    pool.indirect_dma_start(
                        table, bass.IndirectOffsetOnAxis(ap=row_now[:, h, j:j + 1], axis=0),
                        rec_now[:, h, j, :], None).then_inc(scattered[h], 16)

            with pool.Fori(0, STEPS // 2) as i:
                for h in range(2):
                    scatter(2 * i + h, h)

            for l in range(LAYERS):
                first = l * GROUPS
                if l == 0:
                    pool.wait_ge(ln_out, 32 * LN_TILES)
                else:
                    for i in range(2):
                        pool.wait_ge(stored[i], 32 * fills[i] * l)
                pool.wait_ge(prepared, l + 1)

                def gather(k, g):
                    ge(pool, group_done, first + k - 3)
                    pool.wait_ge(staged, first + k + 1)
                    hold(pool)
                    for j in range(2):
                        pool.indirect_dma_start(
                            gath[:, g, j, :], None, split_rows[l],
                            bass.IndirectOffsetOnAxis(ap=idx_now[:, g, j:j + 1], axis=0)
                        ).then_inc(landed[g], 16)

                for g in range(4):
                    gather(g, g)
                if l == 0:
                    pool.wait_ge(unpacked_v, 6)
                    pool.wait_ge(unpacked_a, 6)
                    pool.memset(sums[:, early_end // 2:early_end], 0.0).then_inc(cleared, 1)
                with pool.Fori(1, PASSES) as i:
                    for g in range(4):
                        gather(4 * i + g, g)

                mlp_first = l * BLOCKS
                last = l == LAYERS - 1
                pool.wait_ge(added, (l + 1) * GROUPS)

                def bias_and_clear(b, i, turn, lead, main, trail):
                    if lead:
                        pool.wait_ge(z_loaded[1 - i], 16 * (l * fills[1 - i] + turn + 1))
                        ge(pool, z_ready, mlp_first + b)
                        hold(pool)
                        pool.tensor_tensor(z_bias[1 - i], z_in[1 - i], nb2_row[:, :], ALU.add
                                           ).then_inc(bias_added, 1)
                        if last:
                            pool.wait_ge(bias_added, mlp_first + b + 2)
                            pool.wait_ge(x_loaded[1 - i], 16 * (turn + 1))
                            hold(pool)
                            pool.tensor_tensor(z_bias[1 - i], z_bias[1 - i], x_in[1 - i], ALU.add
                                               ).then_inc(x_added, 1)
                    if trail and not last:
                        ge(pool, hid_summed, mlp_first + b)
                        ge(pool, rel_ready, 4 * (mlp_first + b))
                        hold(pool)
                        pool.tensor_copy(block_sums(b - 1, 0, DCOL), zero_col[:, :].broadcast_to([P, DCOL])
                                         ).then_inc(emptied, 1)

                over_blocks(pool, bias_and_clear)

        @block.vector
        def _(dve):
            dve.wait_ge(consts, 9)
            dve.tensor_copy(iota_f[:, :], iota_i[:, :]).then_inc(consts_v, 1)
            dve.tensor_copy(iota_b[:, :], iota_i[:, 0:P]).then_inc(consts_v, 1)
            dve.wait_ge(src_in, 32)
            dve.tensor_single_scalar(blk_i[:, :], src_i[:, :], 7, ALU.arith_shift_right).then_inc(keyed, 1)
            dve.wait_ge(keyed, 1)
            dve.tensor_copy(blk_b[:, :], blk_i[:, :]).then_inc(keyed, 1)
            dve.tensor_copy(blk_f[:, :], blk_i[:, :]).then_inc(keyed, 1)
            dve.wait_ge(keyed, 3)
            for b in range(BUCKETS):
                ge(dve, counted, b - 1)
                dve.tensor_scalar(same[b % 2], blk_b[:, :], float(b), 0.0, ALU.is_equal, ALU.add,
                                  accum_out=counts[:, b:b + 1]).then_inc(counted, 1)
            dve.wait_ge(edges_in, 64)
            dve.scalar_tensor_tensor(key_f[:, :], dst_i[:, :], float(KEY), src_i[:, :], ALU.mult, ALU.add
                                     ).then_inc(keyed, 1)
            dve.wait_ge(keyed, 4)
            dve.scalar_tensor_tensor(key_f[:, :], blk_f[:, :], float(-P), key_f[:, :], ALU.mult, ALU.add
                                     ).then_inc(keyed, 1)
            dve.wait_ge(totals, 2)
            dve.tensor_scalar(quot_i[0:BUCKETS, 0:1], ps[0][0:BUCKETS, 512:513], float(GROUP - 1), None, ALU.add
                              ).then_inc(quot, 1)
            dve.wait_ge(quot, 1)
            dve.tensor_single_scalar(quot_i[0:BUCKETS, 1:2], quot_i[0:BUCKETS, 0:1], 8, ALU.arith_shift_right
                                     ).then_inc(quot, 1)
            dve.wait_ge(quot, 2)
            dve.tensor_copy(quot_f[0:BUCKETS, :], quot_i[0:BUCKETS, 1:2]).then_inc(quot, 1)
            dve.wait_ge(quot, 3)
            dve.tensor_scalar(quot_rows[0:BUCKETS, :], ones[0:BUCKETS, :], quot_f[0:BUCKETS, 0:1], None, ALU.mult
                              ).then_inc(quot, 1)
            dve.wait_ge(bases, 2)
            dve.tensor_copy(prod[:, 0, :], ps[0][:, 0:BUCKETS]).then_inc(ran, 1)
            dve.wait_ge(ran, 1)
            dve.scalar_tensor_tensor(run[:, 0, 0:BLOCKS], ps[1][:, 0:BLOCKS], float(GROUP), prod[:, 0, 0:BLOCKS],
                                     ALU.mult, ALU.add).then_inc(ran, 1)
            dve.tensor_scalar(run[:, 0, BLOCKS:BUCKETS], prod[:, 0, BLOCKS:BUCKETS], float(GROUPS * GROUP), None,
                              ALU.add).then_inc(ran, 1)
            dve.tensor_copy(quot_f[0:BLOCKS, :], ps[1][0:BLOCKS, 512:513]).then_inc(ran, 1)
            dve.wait_ge(ran, 4)
            dve.wait_ge(consts_v, 2)
            dve.tensor_scalar(started[0:BLOCKS, :], iota_f[0:BLOCKS, :], quot_f[0:BLOCKS, 0:1], None, ALU.is_ge
                              ).then_inc(starts, 1)
            dve.wait_ge(grouped, 1)
            for n in range(2):
                dve.tensor_scalar(group_block[:, n * GROUPS // 2:(n + 1) * GROUPS // 2],
                                  ps[n][0:1, 0:GROUPS // 2], -1.0, None, ALU.add).then_inc(blocks_known, 1)

            def rank(s, h, i):
                done = s * OPS
                ge(dve, ranked, done)
                dve.tensor_tensor(hot[:, :, :],
                                  iota_f[:, 0:BUCKETS].rearrange("p (j b) -> p j b", j=1)
                                  .broadcast_to([P, STEP, BUCKETS]),
                                  blk_f[:, bass.ds(s * STEP, STEP)].rearrange("p (j b) -> p j b", b=1)
                                  .broadcast_to([P, STEP, BUCKETS]), ALU.is_equal).then_inc(ranked, 1)
                for j in range(STEP - 1):
                    dve.wait_ge(ranked, done + 1 + j)
                    dve.tensor_tensor(run[:, j + 1, :], run[:, j, :], hot[:, j, :], ALU.add).then_inc(ranked, 1)
                dve.wait_ge(ranked, done + STEP)
                dve.tensor_tensor(prod[:, :, :], run[:, :, :], hot[:, :, :], ALU.mult).then_inc(ranked, 1)
                dve.wait_ge(ranked, done + STEP + 1)
                dve.tensor_reduce(pos_f[:, :], prod[:, :, :], AXX, ALU.add).then_inc(ranked, 1)
                dve.tensor_tensor(run[:, 0, :], run[:, STEP - 1, :], hot[:, STEP - 1, :], ALU.add
                                  ).then_inc(ranked, 1)
                dve.wait_ge(ranked, done + STEP + 3)
                dve.tensor_copy(pos_i[:, :], pos_f[:, :]).then_inc(ranked, 1)
                dve.wait_ge(ranked, done + STEP + 4)
                dve.tensor_single_scalar(pos_p[:, :], pos_i[:, :], P - 1, ALU.bitwise_and).then_inc(ranked, 1)
                dve.tensor_single_scalar(pos_c[:, :], pos_i[:, :], 7, ALU.arith_shift_right).then_inc(ranked, 1)
                dve.wait_ge(ranked, done + STEP + 6)
                ge(dve, scattered[h], STEP * 16 * i)
                dve.scalar_tensor_tensor(row_now[:, h, :], pos_p[:, :], float(TCOLS), pos_c[:, :],
                                         ALU.mult, ALU.add).then_inc(rows_ready, 1)

            def layernorm(t):
                done = 6 * t
                rows = slice(0, LN_ROWS)
                dve.wait_ge(ln_in, 16 * (t + 1))
                dve.bn_stats(ln_stats[rows, :], ln_x[rows, :]).then_inc(ln_vec, 1)
                dve.wait_ge(ln_vec, done + 1)
                hold(dve)
                dve.bn_aggr(ln_mv[rows, :], ln_stats[rows, :]).then_inc(ln_vec, 1)
                dve.wait_ge(ln_act, 4 * t + 1)
                dve.reciprocal(ln_rstd[rows, :], ln_std[rows, :]).then_inc(ln_vec, 1)
                dve.wait_ge(ln_vec, done + 3)
                dve.tensor_scalar(ln_y[rows, :], ln_x[rows, :], ln_mv[rows, 0:1], ln_rstd[rows, 0:1],
                                  ALU.subtract, ALU.mult).then_inc(ln_vec, 1)
                dve.wait_ge(ln_act, 4 * t + 3)
                dve.tensor_tensor(ln_r[rows, :], ln_z[rows, :], ln_split[rows, 0:H], ALU.subtract
                                  ).then_inc(ln_vec, 1)
                dve.wait_ge(ln_vec, done + 5)
                dve.wait_ge(ln_act, 4 * t + 4)
                dve.tensor_tensor(ln_split[rows, 2 * H:3 * H], ln_r[rows, :], ln_split[rows, H:2 * H],
                                  ALU.subtract).then_inc(ln_vec, 1)

            def four_steps(o):
                for r in range(4):
                    rank(4 * o + r, r % 2, 2 * o + r // 2)
                layernorm(o)

            dve.wait_ge(ran, 4)
            four_steps(0)
            with dve.Fori(1, ROUNDS) as o:
                four_steps(o)
            for t in range(ROUNDS, LN_TILES):
                layernorm(t)

            dve.wait_ge(table_in, 16)
            dve.tensor_copy(key_i[:, :], tab[:, :, 0]).then_inc(unpacked_v, 1)
            dve.wait_ge(unpacked_v, 1)
            dve.tensor_single_scalar(dst_part[:, :], key_i[:, :], 8, ALU.arith_shift_right).then_inc(unpacked_v, 1)
            dve.tensor_single_scalar(node_part[:, :], key_i[:, :], KEY - 1, ALU.bitwise_and
                                     ).then_inc(unpacked_v, 1)
            dve.wait_ge(unpacked_a, 2)
            dve.tensor_tensor(a_rest[:, :], a_all[:, :], parts[:, :, 1], ALU.subtract).then_inc(unpacked_v, 1)
            dve.wait_ge(unpacked_v, 4)
            dve.tensor_copy(local[:, :], node_part[:, :]).then_inc(unpacked_v, 1)
            dve.wait_ge(unpacked_a, 3)
            dve.tensor_tensor(parts[:, :, 3], a_rest[:, :], parts[:, :, 2], ALU.subtract).then_inc(unpacked_v, 1)
            dve.wait_ge(unpacked_v, 6)
            dve.wait_ge(unpacked_a, 6)
            dve.memset(sums[:, 0:early_end // 2], 0.0).then_inc(cleared, 1)

            for l in range(LAYERS):
                dve.wait_ge(weights_in, 16 * W_DMAS * (l + 1))
                done = 19 * l
                rows_of = ((s_row, w_row), (s_col[:, :], w_col[:, :]))
                for s_, w_ in rows_of:
                    dve.tensor_scalar(s_, w_, 0.0, 2.0, ALU.is_ge, ALU.mult).then_inc(prep_v, 1)
                dve.wait_ge(prep_v, done + 2)
                for s_, w_ in rows_of:
                    dve.tensor_scalar(s_, s_, 1.0, None, ALU.subtract).then_inc(prep_v, 1)
                dve.wait_ge(prep_v, done + 4)
                dve.tensor_tensor(m_row, w_row, s_row, ALU.mult).then_inc(prep_v, 1)
                dve.tensor_tensor(b_row, b_row, s_row, ALU.mult).then_inc(prep_v, 1)
                dve.scalar_tensor_tensor(wh_col[:, :], w_col[:, :], 0.5, s_col[:, :], ALU.mult, ALU.mult
                                         ).then_inc(prep_v, 1)
                dve.scalar_tensor_tensor(bh_col[:, :], b_col[:, :], 0.5, s_col[:, :], ALU.mult, ALU.mult
                                         ).then_inc(prep_v, 1)
                dve.wait_ge(prep_v, done + 8)
                dve.tensor_scalar(m_row, m_row, TINY, None, ALU.max).then_inc(prep_v, 1)
                dve.wait_ge(prep_v, done + 9)
                dve.reciprocal(m_row, m_row).then_inc(prep_v, 1)
                dve.wait_ge(prep_v, done + 10)
                dve.scalar_tensor_tensor(thresh[:, :], b_row, -1.0, m_row, ALU.mult, ALU.mult).then_inc(prep_v, 1)
                dve.memset(d_cols[:, 2:4, 1:4], 0.0).then_inc(prep_v, 1)
                for c in range(HC):
                    dve.tensor_scalar(d_cols[:, c, 0:1], b_col[:, c:c + 1], 0.5, None, ALU.mult
                                      ).then_inc(prep_v, 1)
                    dve.tensor_copy(d_cols[:, 2 + c, 0:1], eb2_col[:, c:c + 1]).then_inc(prep_v, 1)
                    dve.tensor_scalar(d_cols[:, c, 1:4], w_col[:, c:c + 1].broadcast_to([P, 3]), 0.5, None,
                                      ALU.mult).then_inc(prep_v, 1)
                dve.wait_ge(ew2_turned, l + 1)
                dve.tensor_copy(ew2_T[:, :, :].rearrange("p c n -> p (c n)"), ps[0][:, 0:HC * H]
                                ).then_inc(ew2_kept, 1)
                dve.wait_ge(we_summed, l + 1)
                dve.tensor_copy(we[:, :, :].rearrange("p c n -> p (c n)"), ps[1][:, 0:HC * H]).then_inc(we_kept, 1)
                dve.wait_ge(wd_summed, l + 1)
                dve.tensor_copy(wd[:, :], ps[0][0:4, 512:512 + H]).then_inc(prep_v, 1)
                dve.wait_ge(prep_v, done + 19)
                dve.wait_ge(we_kept, l + 1)
                dve.sem_inc(prepared, 1)

                first = l * GROUPS
                dve.wait_ge(cleared, 3)
                ge(dve, emptied, l * BLOCKS)

                def one_hots(k, g):
                    ge(dve, group_done, first + k - 1)
                    for j in range(2):
                        t = 2 * k + j
                        to = hots[:, g % 2, j, :]
                        node = local[:, bass.ds(t, 1)]
                        dve.tensor_scalar(to[:, 0:P], iota_b[:, :], node, None, ALU.is_equal)
                        for q in range(1, 4):
                            op = dve.tensor_scalar(to[:, q * P:(q + 1) * P], iota_b[:, :], node,
                                                   parts[:, bass.ds(t, 1), q], ALU.is_equal, ALU.mult)
                    op.then_inc(hots_ready, 1)

                def add(k, g):
                    at = dve.value_load(group_block[0:1, bass.ds(k, 1)], min_val=0, max_val=BLOCKS - 1)
                    n = BCOLS if l == 0 else DCOL
                    ge(dve, added, first + k)
                    dve.wait_ge(group_done, first + k + 1)
                    dve.tensor_tensor(block_sums(at, 0, n), block_sums(at, 0, n), ps[g % 2][:, 0:n], ALU.add
                                      ).then_inc(added, 1)

                def body(i, gs):
                    for g in range(4):
                        if g in gs:
                            one_hots(4 * i + g + 1, g + 1)
                        add(4 * i + g, g)

                one_hots(0, 0)
                body(0, range(4))
                with dve.Fori(1, PASSES - 1) as i:
                    body(i, range(4))
                body(PASSES - 1, range(3))

                mlp_first = l * BLOCKS
                last = l == LAYERS - 1
                dve.wait_ge(added, (l + 1) * GROUPS)

                def mlp(b, i, turn, lead, main, trail):
                    if lead:
                        f = mlp_first + b + 1
                        ge(dve, turned, f - 1)
                        dve.tensor_copy(d_in[:, 1 - i, :], block_sums(b + 1, DCOL, 4)).then_inc(d_taken, 1)
                        dve.wait_ge(turned, f + 1)
                        ge(dve, hid_summed, f - 1)
                        dve.tensor_copy(d_T[1 - i], ps_d[1 - i][0:4, 0:P]).then_inc(dT_ready, 1)
                        ge(dve, rel_ready, 4 * f)
                        for c in range(HC):
                            dve.tensor_scalar(scaled[:, c * P:(c + 1) * P], block_sums(b + 1, 2 * c * P + P, P),
                                              wh_col[:, c:c + 1], None, ALU.mult).then_inc(rel_ready, 1)
                        dve.wait_ge(rel_ready, 4 * f + 2)
                        for c in range(HC):
                            dve.scalar_tensor_tensor(rel[1 - i][:, c * P:(c + 1) * P],
                                                     block_sums(b + 1, 2 * c * P, P), bh_col[:, c:c + 1],
                                                     scaled[:, c * P:(c + 1) * P], ALU.mult, ALU.add
                                                     ).then_inc(rel_ready, 1)
                    if trail:
                        f = mlp_first + b - 1
                        dve.wait_ge(out_summed, f + 1)
                        if last:
                            dve.wait_ge(x_added, b)
                            ge(dve, stored[1 - i], 32 * l * fills[1 - i] + 16 * (turn - 1))
                        else:
                            dve.wait_ge(bias_added, f + 1)
                            ge(dve, stored[1 - i], 32 * (l * fills[1 - i] + turn - 1))
                        dve.tensor_tensor(z_out[1 - i], ps_out[1 - i][:, 0:H], z_bias[1 - i], ALU.add
                                          ).then_inc(z_ready, 1)
                        if not last:
                            dve.wait_ge(hi_ready, f + 1)
                            dve.wait_ge(z_ready, f + 1)
                            dve.tensor_tensor(residue, z_out[1 - i], z_split[1 - i][:, 0:H], ALU.subtract
                                              ).then_inc(res_ready, 1)
                            dve.wait_ge(mid_ready, f + 1)
                            dve.wait_ge(res_ready, f + 1)
                            dve.tensor_tensor(z_split[1 - i][:, 2 * H:3 * H], residue, z_split[1 - i][:, H:2 * H],
                                              ALU.subtract).then_inc(lo_ready, 1)

                over_blocks(dve, mlp)

        @block.scalar
        def _(act):
            def records(s, h, i):
                ge(act, scattered[h], STEP * 16 * i)
                hold(act)
                act.activation(rec_now[:, h, :, 0], key_f[:, bass.ds(s * STEP, STEP)], ACT.Copy)
                act.activation(rec_now[:, h, :, 1], a_e[:, bass.ds(s * STEP, STEP)], ACT.Copy
                               ).then_inc(recs_ready, 1)

            def layernorm(t):
                rows = slice(0, LN_ROWS)
                act.wait_ge(ln_vec, 6 * t + 2)
                act.activation(ln_std[rows, :], ln_mv[rows, 1:2], ACT.Sqrt, bias=eps_col[rows, :]
                               ).then_inc(ln_act, 1)
                act.wait_ge(ln_vec, 6 * t + 4)
                ge(act, ln_out, 32 * t)
                act.activation(ln_z[rows, :], ln_y[rows, :], ACT.Relu).then_inc(ln_act, 1)
                act.activation(ln_split[rows, 0:H], ln_y[rows, :], ACT.Relu).then_inc(ln_act, 1)
                act.wait_ge(ln_vec, 6 * t + 5)
                act.activation(ln_split[rows, H:2 * H], ln_r[rows, :], ACT.Copy).then_inc(ln_act, 1)

            def four_steps(o):
                for r in range(4):
                    records(4 * o + r, r % 2, 2 * o + r // 2)
                layernorm(o)

            act.wait_ge(keyed, 5)
            act.wait_ge(table_filled, 32)
            four_steps(0)
            with act.Fori(1, ROUNDS) as o:
                four_steps(o)
            for t in range(ROUNDS, LN_TILES):
                layernorm(t)

            act.wait_ge(table_in, 16)
            act.activation(a_all[:, :], tab[:, :, 1], ACT.Copy).then_inc(unpacked_a, 1)
            act.activation(parts[:, :, 1], tab[:, :, 1], ACT.Copy).then_inc(unpacked_a, 1)
            act.wait_ge(unpacked_v, 4)
            act.activation(parts[:, :, 2], a_rest[:, :], ACT.Copy).then_inc(unpacked_a, 1)
            act.wait_ge(unpacked_v, 3)
            act.activation(dst_all[:, :], dst_part[:, :], ACT.Copy).then_inc(unpacked_a, 1)
            act.wait_ge(unpacked_a, 4)
            act.sem_inc(unpacked_a, 2)

            for l in range(LAYERS):
                first = l * GROUPS
                act.wait_ge(prepared, l + 1)

                def stage(k, g, i):
                    ge(act, landed[g], 32 * (l * PASSES + i))
                    hold(act)
                    act.activation(idx_now[:, g, :], dst_all[:, bass.ds(2 * k, 2)], ACT.Copy).then_inc(staged, 1)

                def sign_rows(k, g):
                    ge(act, group_done, first + k - 1)
                    hold(act)
                    for j in range(2):
                        op = act.activation(signs[:, g % 2, j, :], thresh[:, :], ACT.Sign,
                                            bias=a_all[:, bass.ds(2 * k + j, 1)], scale=-1.0)
                    op.then_inc(signs_ready, 1)

                for g in range(4):
                    stage(g, g, 0)
                for g in range(4):
                    sign_rows(g, g)
                    stage(4 + g, g, 1)
                with act.Fori(1, PASSES - 1) as i:
                    for g in range(4):
                        sign_rows(4 * i + g, g)
                        stage(4 * i + 4 + g, g, i + 1)
                for g in range(4):
                    sign_rows(GROUPS - 4 + g, g)

                mlp_first = l * BLOCKS
                last = l == LAYERS - 1
                act.wait_ge(added, (l + 1) * GROUPS)

                def mlp(b, i, turn, lead, main, trail):
                    if lead:
                        act.wait_ge(turned, mlp_first + b + 2)
                        ge(act, hid_summed, mlp_first + b)
                        act.activation(z_T[1 - i], ps[1 - i][:, 0:H], ACT.Copy).then_inc(zT_ready, 1)
                    if main:
                        act.wait_ge(hid_summed, mlp_first + b + 1)
                        ge(act, out_summed, mlp_first + b - 1)
                        for c in range(HC):
                            op = act.activation(hid[i][:, c * P:(c + 1) * P],
                                                ps[i][:, 512 + c * P:512 + (c + 1) * P], ACT.Relu,
                                                bias=nb1_col[:, c:c + 1])
                        op.then_inc(hid_ready, 1)
                    if trail and not last:
                        f = mlp_first + b - 1
                        act.wait_ge(z_ready, f + 1)
                        ge(act, stored[1 - i], 32 * (l * fills[1 - i] + turn - 1))
                        act.activation(z_split[1 - i][:, 0:H], z_out[1 - i], ACT.Copy).then_inc(hi_ready, 1)
                        act.wait_ge(res_ready, f + 1)
                        act.activation(z_split[1 - i][:, H:2 * H], residue, ACT.Copy).then_inc(mid_ready, 1)

                over_blocks(act, mlp)

        @block.tensor
        def _(pe):
            pe.wait_ge(consts, 9)
            pe.wait_ge(counted, BUCKETS)
            pe.matmul(ps[0][:, 0:BUCKETS], later[:, :], counts[:, :], start=True, stop=True).then_inc(totals, 1)
            pe.matmul(ps[0][0:BUCKETS, 512:513], counts[:, :], ones[:, 0:1], start=True, stop=True
                      ).then_inc(totals, 1)
            pe.wait_ge(quot, 4)
            pe.matmul(ps[1][:, 0:BUCKETS], quot_rows[0:BUCKETS, :], later[0:BUCKETS, 0:BUCKETS],
                      start=True, stop=True).then_inc(bases, 1)
            pe.matmul(ps[1][0:BUCKETS, 512:513], later[0:BUCKETS, 0:BUCKETS], quot_f[0:BUCKETS, :],
                      start=True, stop=True).then_inc(bases, 1)
            pe.wait_ge(starts, 1)
            for n in range(2):
                op = pe.matmul(ps[n][0:1, 0:GROUPS // 2], ones[0:BLOCKS, 0:1],
                               started[0:BLOCKS, n * GROUPS // 2:(n + 1) * GROUPS // 2], start=True, stop=True)
            op.then_inc(grouped, 1)

            for l in range(LAYERS):
                pe.wait_ge(blocks_known, 2)
                pe.wait_ge(weights_in, 16 * W_DMAS * (l + 1))
                for m in range(HC):
                    for c in range(HC):
                        op = pe.transpose(ps[0][:, m * H + c * P:m * H + (c + 1) * P],
                                          ew2_in[:, c, m * P:(m + 1) * P], ident[:, :])
                op.then_inc(ew2_turned, 1)
                pe.wait_ge(ew2_kept, l + 1)
                for c in range(HC):
                    for m in range(HC):
                        op = pe.matmul(ps[1][:, c * H:(c + 1) * H], ew2_T[:, m, c * P:(c + 1) * P], wa[:, m, :],
                                       start=(m == 0), stop=(m == HC - 1))
                op.then_inc(we_summed, 1)
                pe.wait_ge(we_kept, l + 1)
                pe.wait_ge(prep_v, 19 * l + 18)
                for c in range(HC):
                    pe.matmul(ps[0][0:4, 512:512 + H], d_cols[:, c, :], we[:, c, :], start=(c == 0), stop=False)
                for c in range(HC):
                    op = pe.matmul(ps[0][0:4, 512:512 + H], d_cols[:, 2 + c, :], wa[:, c, :], start=False,
                                   stop=(c == HC - 1))
                op.then_inc(wd_summed, 1)
                pe.wait_ge(prepared, l + 1)

                first = l * GROUPS

                def group(k, g, i):
                    pe.wait_ge(hots_ready, first + k + 1)
                    pe.wait_ge(signs_ready, first + k + 1)
                    ge(pe, added, first + k - 1)
                    acc = ps[g % 2]
                    for j in range(2):
                        hot_j = hots[:, g % 2, j, :]
                        for c in range(HC):
                            sg = signs[:, g % 2, j, c * P:(c + 1) * P]
                            o = 2 * c * P
                            pe.matmul(acc[:, o:o + 2 * P], sg, hot_j[:, 0:2 * P],
                                      start=(j == 0 and c == 0), stop=False, skip_group_check=True)
                            for q in (2, 3):
                                pe.matmul(acc[:, o + P:o + 2 * P], sg, hot_j[:, q * P:(q + 1) * P],
                                          start=False, stop=(j == 1 and q == 3), skip_group_check=True)
                    pe.wait_ge(landed[g], 32 * (l * PASSES + i + 1))
                    for j in range(2):
                        hot_j = hots[:, g % 2, j, :]
                        for c in range(HC):
                            for q in range(3):
                                op = pe.matmul(acc[:, XCOL + c * P:XCOL + (c + 1) * P],
                                               gath[:, g, j, q * H + c * P:q * H + (c + 1) * P], hot_j[:, 0:P],
                                               start=(j == 0 and c == 0 and q == 0),
                                               stop=(j == 1 and q == 2), skip_group_check=True)
                        if l == 0:
                            op = pe.matmul(acc[:, DCOL:DCOL + 4], hot_j[:, 0:P],
                                           parts[:, bass.ds(2 * k + j, 1), :].rearrange("p t q -> p (t q)"),
                                           start=False, stop=(j == 1), skip_group_check=True)
                    op.then_inc(group_done, 1)

                for g in range(4):
                    group(g, g, 0)
                with pe.Fori(1, PASSES) as i:
                    for g in range(4):
                        group(4 * i + g, g, i)

                mlp_first = l * BLOCKS
                last = l == LAYERS - 1
                pe.wait_ge(added, (l + 1) * GROUPS)

                def mlp(b, i, turn, lead, main, trail):
                    if lead:
                        f = mlp_first + b + 1
                        pe.wait_ge(z_loaded[1 - i], 16 * (l * fills[1 - i] + turn + 1))
                        pe.wait_ge(d_taken, f + 1)
                        ge(pe, zT_ready, f - 1)
                        ge(pe, dT_ready, f - 1)
                        for c in range(HC):
                            pe.transpose(ps[1 - i][:, c * P:(c + 1) * P], z_in[1 - i][:, c * P:(c + 1) * P],
                                         ident[:, :])
                        pe.transpose(ps_d[1 - i][0:4, 0:P], d_in[:, 1 - i, :], ident[:, :]
                                     ).then_inc(turned, 1)
                    if main:
                        f = mlp_first + b
                        pe.wait_ge(zT_ready, f + 1)
                        pe.wait_ge(dT_ready, f + 1)
                        pe.wait_ge(rel_ready, 4 * (f + 1))
                        ge(pe, hid_ready, f - 1)
                        ge(pe, z_ready, f - 1)
                        for n in range(HC):
                            fs = slice(n * P, (n + 1) * P)
                            to = ps[i][:, 512 + n * P:512 + (n + 1) * P]
                            for c in range(HC):
                                pe.matmul(to, wa[:, c, fs], block_sums(b, XCOL + c * P, P), start=(c == 0),
                                          stop=False)
                                pe.matmul(to, wx[:, c, fs], z_T[i][:, c * P:(c + 1) * P], start=False, stop=False)
                                pe.matmul(to, we[:, c, fs], rel[i][:, c * P:(c + 1) * P], start=False, stop=False)
                            op = pe.matmul(to, wd[:, fs], d_T[i], start=False, stop=True)
                        op.then_inc(hid_summed, 1)
                    if trail:
                        f = mlp_first + b - 1
                        pe.wait_ge(hid_ready, f + 1)
                        for c in range(HC):
                            op = pe.matmul(ps_out[1 - i][:, 0:H], hid[1 - i][:, c * P:(c + 1) * P], w2[:, c, :],
                                           start=(c == 0), stop=(c == HC - 1))
                        op.then_inc(out_summed, 1)

                over_blocks(pe, mlp)


_LAYER = ("eW1", "eb1", "eW2", "eb2", "nW1", "nb1", "nW2", "nb2")


def kernel(**inputs):
    import numpy as _np
    import concourse.bacc as _bacc
    from concourse import mybir as _mybir
    from concourse.bass_utils import run_bass_kernel_spmd as _run

    nc = _bacc.Bacc("TRN2", target_bir_lowering=False, num_devices=1)
    arrays = {}

    def given(name):
        a = _np.ascontiguousarray(inputs[name])
        arrays[f"in_{name}"] = a
        return nc.dram_tensor(f"in_{name}", a.shape, _mybir.dt.from_np(a.dtype), kind="ExternalInput").ap()

    edges = [given(name) for name in ("x", "src", "dst", "edge_weight1")]
    weights = [[given(f"L0_gnn_l{l}_{name}") for l in range(LAYERS)] for name in _LAYER]
    out = nc.dram_tensor("out_0", (N_NODES, H), _mybir.dt.float32, kind="ExternalOutput").ap()
    gnn(nc, *edges, *weights, out)
    r = _run(nc, [arrays], core_ids=[0])
    return r.results[0]["out_0"]
```

```python
from contextlib import ExitStack

import concourse.bass as bass
from concourse import mybir

F32 = mybir.dt.float32
BF16 = mybir.dt.bfloat16
I32 = mybir.dt.int32
U32 = mybir.dt.uint32
U16 = mybir.dt.uint16
U8 = mybir.dt.uint8
I16 = mybir.dt.int16
ALU = mybir.AluOpType
ACT = mybir.ActivationFunctionType
AXX = mybir.AxisListType.X

P = 128
N_NODES = 6250
N_EDGES = 200000
H = 256
HC = H // P
LAYERS = 2
EPS = 1e-5
TINY = 1e-30

BLOCKS = -(-N_NODES // P)
BUCKETS = BLOCKS + 1
GROUP = 2 * P
GROUPS = -(-(N_EDGES // GROUP + BLOCKS) // 4) * 4
TILES = 2 * GROUPS
PASSES = GROUPS // 4

STEP = 8
ECOLS = -(-N_EDGES // (P * 4 * STEP)) * 4 * STEP
STEPS = ECOLS // STEP
ROUNDS = STEPS // 4
FULL_P = N_EDGES // ECOLS
LAST_C = N_EDGES - FULL_P * ECOLS
TCOLS = TILES + -(-(P * ECOLS - N_EDGES) // P)
FILL_REPS = 10
FILL_COLS = TCOLS // FILL_REPS
KEY = 256
NO_NODE = P
LN_ROWS = 125
LN_TILES = N_NODES // LN_ROWS
LAST_ROWS = N_NODES - (BLOCKS - 1) * P

XCOL = HC * 2 * P
DCOL = XCOL + HC * P
BCOLS = DCOL + 2
PAIRS = (BLOCKS + 1) // 2
assert PAIRS % 2 == 1
OPS = 14


def ge(eng, sem, value):
    if not (isinstance(value, int) and value <= 0):
        eng.wait_ge(sem, value)


def hold(eng):
    eng.nop(nofuse=True)


def over_pairs(eng, step):
    step(-1, 1, 0, True, False, False)
    step(0, 0, 0, True, True, False)
    step(1, 1, 1, True, True, True)
    step(2, 0, 1, True, True, True)
    with eng.Fori(0, (PAIRS - 7) // 2) as n:
        step(2 * n + 3, 1, n + 2, True, True, True)
        step(2 * n + 4, 0, n + 2, True, True, True)
    for q in range(PAIRS - 4, PAIRS):
        step(q, q % 2, (q + 1) // 2, q + 1 < PAIRS, True, True)
    step(PAIRS, 1, (PAIRS + 1) // 2, False, False, True)


def blocks_of(q):
    return BLOCKS - 2 * q if isinstance(q, int) and q == PAIRS - 1 else 2


def gnn(nc, x, src, dst, ew, eW1, eb1, eW2, eb2, nW1, nb1, nW2, nb2, out):
    table = nc.dram_tensor("sorted_edges", [P * TCOLS, 2], F32, kind="Internal").ap()
    z_rows = nc.dram_tensor("z_rows", [BLOCKS * P, H], F32, kind="Internal").ap()
    split_rows = [nc.dram_tensor(f"split_rows{l}", [rows, 3 * H], BF16, kind="Internal").ap()
                  for l, rows in enumerate((N_NODES, BLOCKS * P))]
    with ExitStack() as ctx:
        def sb(name, shape, dt):
            return ctx.enter_context(nc.sbuf_tensor(name, shape, dt))

        def sem(name):
            return ctx.enter_context(nc.semaphore(name))

        sums = sb("sums", [P, BLOCKS * BCOLS], F32)
        dst_all = sb("dst_all", [P, TILES], U16)
        a_all = sb("a_all", [P, TILES], F32)
        parts = sb("parts", [P, TILES, 2], BF16)
        third = sb("third", [P, TILES], F32)
        local = sb("local", [P, TILES], U8)
        work = sb("work", [P, 4608], F32)
        spare = sb("spare", [P, 2 * H], F32)
        thresh = spare[:, 0:H]
        wx = sb("wx", [P, HC, H], F32)
        wa = sb("wa", [P, HC, H], F32)
        we = sb("we", [P, HC, H], F32)
        w2 = sb("w2", [P, HC, H], F32)
        wd = sb("wd", [2, H], F32)
        nb2_row = sb("nb2_row", [P, H], F32)
        w_col = sb("w_col", [P, HC], F32)
        b_col = sb("b_col", [P, HC], F32)
        eb2_col = sb("eb2_col", [P, HC], F32)
        nb1_col = sb("nb1_col", [P, HC], F32)
        s_col = sb("s_col", [P, HC], F32)
        wh_col = sb("wh_col", [P, HC], F32)
        bh_col = sb("bh_col", [P, HC], F32)
        iota_b = sb("iota_b", [P, P], BF16)
        ident = sb("ident", [P, P], F32)
        d_in = sb("d_in", [P, 2, 2, 2], F32)
        zero_col = sb("zero_col", [P, 1], F32)
        eps_col = sb("eps_col", [P, 1], F32)
        ones_b = sb("ones_b", [P, 1], BF16)
        d_T = sb("d_T", [2, 2, 2 * P], F32)
        group_block = sb("group_block", [1, GROUPS], I16)
        idx_now = sb("idx_now", [P, 4, 2], U32)

        gath = work[:, 0:3072].bitcast(BF16).rearrange("p (g j n) -> p g j n", g=4, j=2)
        hots = work[:, 3072:4096].bitcast(BF16).rearrange("p (g j n) -> p g j n", g=2, j=2)
        signs = work[:, 4096:4608].bitcast(BF16).rearrange("p (g j n) -> p g j n", g=2, j=2)
        ew2_in = work[:, 0:512].rearrange("p (c n) -> p c n", c=HC)
        ew2_T = work[:, 512:1024].rearrange("p (c n) -> p c n", c=HC)
        d_cols = work[:, 1024:1032].rearrange("p (c n) -> p c n", c=4)
        w_row, b_row, s_row, m_row = (work[:, 3072 + H * k:3072 + H * k + H] for k in range(4))

        def two(start, n):
            return [work[:, start + n * i:start + n * i + n] for i in range(2)]

        def by_block(v):
            return v.rearrange("p (j n) -> p j n", j=2)

        z_in = [by_block(v) for v in two(0, 2 * H)]
        z_out = [by_block(v) for v in two(4 * H, 2 * H)]
        hid = two(8 * H, 2 * H)
        z_split = [by_block(v.bitcast(BF16)) for v in two(12 * H, 3 * H)]
        x_in = [by_block(v) for v in two(12 * H, 2 * H)]
        residue = by_block(spare[:, :])

        taken = [0]

        def early(n, dt=F32):
            v = sums[:, taken[0]:taken[0] + n]
            taken[0] += n
            return v if dt == F32 else v.bitcast(dt)

        src_i = early(ECOLS, I32)
        dst_i = early(ECOLS, I32)
        a_e = early(ECOLS)
        blk_i = early(ECOLS, I32)
        blk_f = early(ECOLS)
        key_f = early(ECOLS)
        blk_b = early(ECOLS // 2, BF16)
        same = [early(ECOLS // 2, BF16) for _ in range(2)]
        fill = early(2 * FILL_COLS).rearrange("p (c w) -> p c w", w=2)
        iota_i = early(GROUPS, I32)
        iota_f = early(GROUPS)
        started = early(GROUPS)
        later = early(P)
        ones = early(P)
        counts = early(BUCKETS)
        quot_f = early(1)
        quot_i = early(2, I32)
        quot_rows = early(P)
        run = early(STEP * BUCKETS).rearrange("p (j b) -> p j b", j=STEP)
        hot = early(STEP * BUCKETS).rearrange("p (j b) -> p j b", j=STEP)
        prod = early(STEP * BUCKETS).rearrange("p (j b) -> p j b", j=STEP)
        pos_f = early(STEP)
        pos_i = early(STEP, I32)
        pos_p = early(STEP, I32)
        pos_c = early(STEP, I32)
        row_now = early(2 * STEP, U32).rearrange("p (h j) -> p h j", h=2)
        rec_now = early(4 * STEP).rearrange("p (h j w) -> p h j w", h=2, w=2)
        ln_x = early(H)
        ln_y = early(H)
        ln_z = early(H)
        ln_r = early(H)
        ln_split = early(3 * H // 2, BF16)
        ln_stats = early(6)
        ln_mv = early(2)
        ln_std = early(1)
        ln_rstd = early(1)
        early_end = taken[0]
        tab = sums[:, 0:2 * TILES].rearrange("p (t w) -> p t w", w=2)
        key_i = sums[:, 2 * TILES:3 * TILES].bitcast(I32)
        dst_part = sums[:, 3 * TILES:4 * TILES].bitcast(I32)
        node_part = sums[:, 4 * TILES:5 * TILES].bitcast(I32)
        a_rest = sums[:, 5 * TILES:6 * TILES]
        assert 6 * TILES <= early_end

        def block_sums(b, start, n):
            return sums[:, bass.ds(b * BCOLS + start, n)]

        by_blocks = sums[:, :].rearrange("p (b n) -> p b n", n=BCOLS)

        def pair_sums(q, start, n):
            return by_blocks[:, bass.ds(2 * q, blocks_of(q)), start:start + n]

        ps = [ctx.enter_context(nc.psum_tensor(f"ps{i}", [P, 1024], F32)) for i in range(2)]
        ps_d = [ctx.enter_context(nc.psum_tensor(f"ps_d{i}", [P, 512], F32)) for i in range(2)]
        ps_out = [ctx.enter_context(nc.psum_tensor(f"ps_out{i}", [P, 512], F32)) for i in range(2)]

        pads_set, src_in, edges_in, table_filled, consts, consts_v = map(
            sem, "pads_set src_in edges_in table_filled consts consts_v".split())
        keyed, counted, totals, quot, bases, ran, starts, grouped, blocks_known = map(
            sem, "keyed counted totals quot bases ran starts grouped blocks_known".split())
        ranked, rows_ready, recs_ready, table_in = map(
            sem, "ranked rows_ready recs_ready table_in".split())
        scattered = [sem("scattered0"), sem("scattered1")]
        ln_in, ln_vec, ln_act, ln_out = map(sem, "ln_in ln_vec ln_act ln_out".split())
        unpacked_v, unpacked_a, cleared = map(sem, "unpacked_v unpacked_a cleared".split())
        weights_in, prep_v, ew2_turned, ew2_kept, we_summed, we_kept, wd_summed, prepared = map(
            sem, "weights_in prep_v ew2_turned ew2_kept we_summed we_kept wd_summed prepared".split())
        staged, nodes_ready, thirds_ready, hots_ready, signs_ready, group_done, added = map(
            sem, "staged nodes_ready thirds_ready hots_ready signs_ready group_done added".split())
        landed = [sem(f"landed{g}") for g in range(4)]
        turned, zT_ready, dT_ready, rel_ready, hid_summed, hid_ready, out_summed = map(
            sem, "turned zT_ready dT_ready rel_ready hid_summed hid_ready out_summed".split())
        d_taken, scaled, bias_added, z_ready, hi_ready, res_ready, mid_ready, lo_ready = map(
            sem, "d_taken scaled bias_added z_ready hi_ready res_ready mid_ready lo_ready".split())
        x_added, emptied = sem("x_added"), sem("emptied")
        z_loaded, x_loaded, stored = ([sem(f"{n}{i}") for i in range(2)] for n in ("z_loaded", "x_loaded", "stored"))
        fills = [(PAIRS + 1) // 2, PAIRS // 2]

        block = ctx.enter_context(nc.Block())
        W_DMAS = 11

        def flat(v):
            return v.rearrange("a n -> (a n)")

        def everywhere(v):
            return v.rearrange("(a n) -> a n", a=1).broadcast_to([P, H])

        @block.sync
        def _(sp):
            def edges(dest, v, done):
                sp.dma_start(dest[0:FULL_P, :], v[0:FULL_P * ECOLS].rearrange("(p c) -> p c", c=ECOLS)
                             ).then_inc(done, 16)
                sp.dma_start(dest[FULL_P:FULL_P + 1, 0:LAST_C],
                             v[FULL_P * ECOLS:N_EDGES].rearrange("(p c) -> p c", p=1)).then_inc(done, 16)

            sp.wait_ge(pads_set, 4)
            edges(src_i, src, src_in)
            edges(dst_i, dst, edges_in)
            edges(a_e, ew.rearrange("e w -> (e w)"), edges_in)
            sp.dma_start(table.rearrange("(p r n) w -> p r (n w)", p=P, r=FILL_REPS),
                         fill[:, :, :].rearrange("p (r c) w -> p r (c w)", r=1)
                         .broadcast_to([P, FILL_REPS, 2 * FILL_COLS])).then_inc(table_filled, 16)
            sp.dma_start(z_rows[N_NODES:BLOCKS * P, :], ln_z[0:BLOCKS * P - N_NODES, :]
                         ).then_inc(table_filled, 16)

            def layernorm(t):
                ge(sp, ln_vec, 6 * t)
                sp.dma_start(ln_x[0:LN_ROWS, :], x[bass.ds(t * LN_ROWS, LN_ROWS), :]).then_inc(ln_in, 16)
                sp.wait_ge(ln_vec, 6 * t + 6)
                sp.dma_start(z_rows[bass.ds(t * LN_ROWS, LN_ROWS), :], ln_z[0:LN_ROWS, :]
                             ).then_inc(ln_out, 16)
                sp.dma_start(split_rows[0][bass.ds(t * LN_ROWS, LN_ROWS), :], ln_split[0:LN_ROWS, :]
                             ).then_inc(ln_out, 16)

            def weights(l):
                for dest, v in ((w_row, flat(eW1[l])), (b_row, eb1[l]), (nb2_row[:, :], nb2[l])):
                    sp.dma_start(dest, everywhere(v)).then_inc(weights_in, 16)
                for dest, v in ((w_col, flat(eW1[l])), (b_col, eb1[l]), (eb2_col, eb2[l]), (nb1_col, nb1[l])):
                    sp.dma_start(dest[:, :], v.rearrange("(c p) -> p c", p=P),
                                 allow_slow_non_contiguous=True).then_inc(weights_in, 16)
                for dest, v in ((wx, nW1[l][0:H, :]), (wa, nW1[l][H:2 * H, :]), (w2, nW2[l]), (ew2_in, eW2[l])):
                    sp.dma_start(dest[:, :, :], v.rearrange("(c p) n -> p c n", p=P)).then_inc(weights_in, 16)

            weights(0)
            sp.wait_ge(table_filled, 32)
            layernorm(0)
            with sp.Fori(1, LN_TILES) as t:
                layernorm(t)
            for h in range(2):
                sp.wait_ge(scattered[h], STEPS // 2 * STEP * 16)
            sp.dma_start(tab, table.rearrange("(p t) w -> p t w", p=P)[:, 0:TILES, :]).then_inc(table_in, 16)

            for l in range(LAYERS):
                first = l * PAIRS
                last = l == LAYERS - 1
                sp.wait_ge(added, (l + 1) * GROUPS)

                def rows(dram, q):
                    n = blocks_of(q)
                    return dram[bass.ds(q * 2 * P, n * P), :].rearrange("(j p) n -> p j n", p=P), n

                def load_rows(q, i):
                    ge(sp, bias_added, first + q - 1)
                    ge(sp, turned, first + q - 1)
                    v, n = rows(z_rows, q)
                    sp.dma_start(z_in[i][:, 0:n, :], v).then_inc(z_loaded[i], 16)
                    if last:
                        ge(sp, x_added, q - 1)
                        if n == 1:
                            sp.dma_start(x_in[i][0:LAST_ROWS, 0, :], x[N_NODES - LAST_ROWS:N_NODES, :]
                                         ).then_inc(x_loaded[i], 16)
                        else:
                            sp.dma_start(x_in[i][:, :, :], rows(x, q)[0]).then_inc(x_loaded[i], 16)

                def mlp_io(q, i, turn, lead, main, trail):
                    if not isinstance(q, int) or q + 2 < PAIRS:
                        load_rows(q + 2, i)
                    if trail:
                        if last:
                            ge(sp, z_ready, first + q)
                            if blocks_of(q - 1) == 1:
                                sp.dma_start(out[N_NODES - LAST_ROWS:N_NODES, :], z_out[1 - i][0:LAST_ROWS, 0, :]
                                             ).then_inc(stored[1 - i], 16)
                            else:
                                sp.dma_start(rows(out, q - 1)[0], z_out[1 - i][:, :, :]
                                             ).then_inc(stored[1 - i], 16)
                        else:
                            ge(sp, lo_ready, q)
                            v, n = rows(z_rows, q - 1)
                            sp.dma_start(v, z_out[1 - i][:, 0:n, :]).then_inc(stored[1 - i], 16)
                            sp.dma_start(rows(split_rows[l + 1], q - 1)[0], z_split[1 - i][:, 0:n, :]
                                         ).then_inc(stored[1 - i], 16)

                load_rows(0, 0)
                over_pairs(sp, mlp_io)
                for i in range(2):
                    sp.wait_ge(stored[i], fills[i] * (32 * l + (16 if last else 32)))
                if not last:
                    weights(l + 1)

        @block.gpsimd
        def _(pool):
            tail = slice(P // 4 * 3, P)
            pool.memset(src_i[tail, LAST_C:ECOLS], BLOCKS * P).then_inc(pads_set, 1)
            pool.memset(dst_i[tail, LAST_C:ECOLS], 0).then_inc(pads_set, 1)
            pool.memset(a_e[tail, LAST_C:ECOLS], 0.0).then_inc(pads_set, 1)
            pool.wait_ge(pads_set, 3)
            pool.memset(fill[:, :, 0:1], float(NO_NODE)).then_inc(consts, 1)
            pool.memset(fill[:, :, 1:2], 0.0).then_inc(consts, 1)
            pool.memset(ln_z[:, :], 0.0).then_inc(consts, 1)
            pool.memset(ones[:, :], 1.0).then_inc(consts, 1)
            pool.memset(zero_col[:, :], 0.0).then_inc(consts, 1)
            pool.memset(eps_col[:, :], EPS).then_inc(consts, 1)
            pool.iota(iota_i[:, :], pattern=[[1, GROUPS]], base=0, channel_multiplier=0).then_inc(consts, 1)
            pool.wait_ge(consts, 7)
            pool.sem_inc(pads_set, 1)
            pool.affine_select(out=later[:, :], in_=ones[:, :], compare_op=ALU.is_gt, fill=0.0, base=0,
                               pattern=[[1, P]], channel_multiplier=-1).then_inc(consts, 1)
            pool.affine_select(out=ident[:, :], in_=ones[:, :], compare_op=ALU.is_equal, fill=0.0, base=0,
                               pattern=[[1, P]], channel_multiplier=-1).then_inc(consts, 1)
            pool.memset(ones_b[:, :], 1.0).then_inc(consts, 1)
            pool.memset(sums[:, early_end:BLOCKS * BCOLS], 0.0).then_inc(cleared, 1)
            pool.wait_ge(table_filled, 32)

            def scatter(s, h):
                pool.wait_ge(rows_ready, s + 1)
                pool.wait_ge(recs_ready, s + 1)
                hold(pool)
                for j in range(STEP):
                    pool.indirect_dma_start(
                        table, bass.IndirectOffsetOnAxis(ap=row_now[:, h, j:j + 1], axis=0),
                        rec_now[:, h, j, :], None).then_inc(scattered[h], 16)

            with pool.Fori(0, STEPS // 2) as i:
                for h in range(2):
                    scatter(2 * i + h, h)

            for l in range(LAYERS):
                first = l * GROUPS
                if l == 0:
                    pool.wait_ge(ln_out, 32 * LN_TILES)
                else:
                    for i in range(2):
                        pool.wait_ge(stored[i], 32 * fills[i] * l)
                pool.wait_ge(prepared, l + 1)

                def gather(k, g):
                    ge(pool, group_done, first + k - 3)
                    pool.wait_ge(staged, first + k + 1)
                    hold(pool)
                    for j in range(2):
                        pool.indirect_dma_start(
                            gath[:, g, j, :], None, split_rows[l],
                            bass.IndirectOffsetOnAxis(ap=idx_now[:, g, j:j + 1], axis=0)
                        ).then_inc(landed[g], 16)

                for g in range(4):
                    gather(g, g)
                if l == 0:
                    pool.wait_ge(unpacked_v, 6)
                    pool.wait_ge(unpacked_a, 6)
                    pool.memset(sums[:, early_end // 2:early_end], 0.0).then_inc(cleared, 1)
                with pool.Fori(1, PASSES) as i:
                    for g in range(4):
                        gather(4 * i + g, g)

                mlp_first = l * PAIRS
                last = l == LAYERS - 1
                pool.wait_ge(added, (l + 1) * GROUPS)

                def add_bias(q, i, turn, lead, main, trail):
                    if lead:
                        n = blocks_of(q + 1)
                        to = z_out[1 - i][:, 0:n, :]
                        pool.wait_ge(z_loaded[1 - i], 16 * (l * fills[1 - i] + turn + 1))
                        ge(pool, stored[1 - i], l * fills[1 - i] * 32 + turn * (16 if last else 32))
                        hold(pool)
                        pool.tensor_tensor(to, z_in[1 - i][:, 0:n, :],
                                           nb2_row[:, :].rearrange("p (j n) -> p j n", j=1).broadcast_to([P, n, H]),
                                           ALU.add).then_inc(bias_added, 1)
                        if last:
                            pool.wait_ge(bias_added, mlp_first + q + 2)
                            pool.wait_ge(x_loaded[1 - i], 16 * (turn + 1))
                            hold(pool)
                            pool.tensor_tensor(to, to, x_in[1 - i][:, 0:n, :], ALU.add).then_inc(x_added, 1)

                over_pairs(pool, add_bias)

        @block.vector
        def _(dve):
            dve.wait_ge(consts, 9)
            dve.tensor_copy(iota_f[:, :], iota_i[:, :]).then_inc(consts_v, 1)
            dve.tensor_copy(iota_b[:, :], iota_i[:, 0:P]).then_inc(consts_v, 1)
            dve.wait_ge(src_in, 32)
            dve.tensor_single_scalar(blk_i[:, :], src_i[:, :], 7, ALU.arith_shift_right).then_inc(keyed, 1)
            dve.wait_ge(keyed, 1)
            dve.tensor_copy(blk_b[:, :], blk_i[:, :]).then_inc(keyed, 1)
            dve.tensor_copy(blk_f[:, :], blk_i[:, :]).then_inc(keyed, 1)
            dve.wait_ge(keyed, 3)
            for b in range(BUCKETS):
                ge(dve, counted, b - 1)
                dve.tensor_scalar(same[b % 2], blk_b[:, :], float(b), 0.0, ALU.is_equal, ALU.add,
                                  accum_out=counts[:, b:b + 1]).then_inc(counted, 1)
            dve.wait_ge(edges_in, 64)
            dve.scalar_tensor_tensor(key_f[:, :], dst_i[:, :], float(KEY), src_i[:, :], ALU.mult, ALU.add
                                     ).then_inc(keyed, 1)
            dve.wait_ge(keyed, 4)
            dve.scalar_tensor_tensor(key_f[:, :], blk_f[:, :], float(-P), key_f[:, :], ALU.mult, ALU.add
                                     ).then_inc(keyed, 1)
            dve.wait_ge(totals, 2)
            dve.tensor_scalar(quot_i[0:BUCKETS, 0:1], ps[0][0:BUCKETS, 512:513], float(GROUP - 1), None, ALU.add
                              ).then_inc(quot, 1)
            dve.wait_ge(quot, 1)
            dve.tensor_single_scalar(quot_i[0:BUCKETS, 1:2], quot_i[0:BUCKETS, 0:1], 8, ALU.arith_shift_right
                                     ).then_inc(quot, 1)
            dve.wait_ge(quot, 2)
            dve.tensor_copy(quot_f[0:BUCKETS, :], quot_i[0:BUCKETS, 1:2]).then_inc(quot, 1)
            dve.wait_ge(quot, 3)
            dve.tensor_scalar(quot_rows[0:BUCKETS, :], ones[0:BUCKETS, :], quot_f[0:BUCKETS, 0:1], None, ALU.mult
                              ).then_inc(quot, 1)
            dve.wait_ge(bases, 2)
            dve.tensor_copy(prod[:, 0, :], ps[0][:, 0:BUCKETS]).then_inc(ran, 1)
            dve.wait_ge(ran, 1)
            dve.scalar_tensor_tensor(run[:, 0, 0:BLOCKS], ps[1][:, 0:BLOCKS], float(GROUP), prod[:, 0, 0:BLOCKS],
                                     ALU.mult, ALU.add).then_inc(ran, 1)
            dve.tensor_scalar(run[:, 0, BLOCKS:BUCKETS], prod[:, 0, BLOCKS:BUCKETS], float(GROUPS * GROUP), None,
                              ALU.add).then_inc(ran, 1)
            dve.tensor_copy(quot_f[0:BLOCKS, :], ps[1][0:BLOCKS, 512:513]).then_inc(ran, 1)
            dve.wait_ge(ran, 4)
            dve.wait_ge(consts_v, 2)
            dve.tensor_scalar(started[0:BLOCKS, :], iota_f[0:BLOCKS, :], quot_f[0:BLOCKS, 0:1], None, ALU.is_ge
                              ).then_inc(starts, 1)
            dve.wait_ge(grouped, 1)
            for n in range(2):
                dve.tensor_scalar(group_block[:, n * GROUPS // 2:(n + 1) * GROUPS // 2],
                                  ps[n][0:1, 0:GROUPS // 2], -1.0, None, ALU.add).then_inc(blocks_known, 1)

            def rank(s, h, i):
                done = s * OPS
                ge(dve, ranked, done)
                dve.tensor_tensor(hot[:, :, :],
                                  iota_f[:, 0:BUCKETS].rearrange("p (j b) -> p j b", j=1)
                                  .broadcast_to([P, STEP, BUCKETS]),
                                  blk_f[:, bass.ds(s * STEP, STEP)].rearrange("p (j b) -> p j b", b=1)
                                  .broadcast_to([P, STEP, BUCKETS]), ALU.is_equal).then_inc(ranked, 1)
                for j in range(STEP - 1):
                    dve.wait_ge(ranked, done + 1 + j)
                    dve.tensor_tensor(run[:, j + 1, :], run[:, j, :], hot[:, j, :], ALU.add).then_inc(ranked, 1)
                dve.wait_ge(ranked, done + STEP)
                dve.tensor_tensor(prod[:, :, :], run[:, :, :], hot[:, :, :], ALU.mult).then_inc(ranked, 1)
                dve.wait_ge(ranked, done + STEP + 1)
                dve.tensor_reduce(pos_f[:, :], prod[:, :, :], AXX, ALU.add).then_inc(ranked, 1)
                dve.tensor_tensor(run[:, 0, :], run[:, STEP - 1, :], hot[:, STEP - 1, :], ALU.add
                                  ).then_inc(ranked, 1)
                dve.wait_ge(ranked, done + STEP + 3)
                dve.tensor_copy(pos_i[:, :], pos_f[:, :]).then_inc(ranked, 1)
                dve.wait_ge(ranked, done + STEP + 4)
                dve.tensor_single_scalar(pos_p[:, :], pos_i[:, :], P - 1, ALU.bitwise_and).then_inc(ranked, 1)
                dve.tensor_single_scalar(pos_c[:, :], pos_i[:, :], 7, ALU.arith_shift_right).then_inc(ranked, 1)
                dve.wait_ge(ranked, done + STEP + 6)
                ge(dve, scattered[h], STEP * 16 * i)
                dve.scalar_tensor_tensor(row_now[:, h, :], pos_p[:, :], float(TCOLS), pos_c[:, :],
                                         ALU.mult, ALU.add).then_inc(rows_ready, 1)

            def layernorm(t):
                done = 6 * t
                rows = slice(0, LN_ROWS)
                dve.wait_ge(ln_in, 16 * (t + 1))
                dve.bn_stats(ln_stats[rows, :], ln_x[rows, :]).then_inc(ln_vec, 1)
                dve.wait_ge(ln_vec, done + 1)
                hold(dve)
                dve.bn_aggr(ln_mv[rows, :], ln_stats[rows, :]).then_inc(ln_vec, 1)
                dve.wait_ge(ln_act, 4 * t + 1)
                dve.reciprocal(ln_rstd[rows, :], ln_std[rows, :]).then_inc(ln_vec, 1)
                dve.wait_ge(ln_vec, done + 3)
                dve.tensor_scalar(ln_y[rows, :], ln_x[rows, :], ln_mv[rows, 0:1], ln_rstd[rows, 0:1],
                                  ALU.subtract, ALU.mult).then_inc(ln_vec, 1)
                dve.wait_ge(ln_act, 4 * t + 3)
                dve.tensor_tensor(ln_r[rows, :], ln_z[rows, :], ln_split[rows, 0:H], ALU.subtract
                                  ).then_inc(ln_vec, 1)
                dve.wait_ge(ln_vec, done + 5)
                dve.wait_ge(ln_act, 4 * t + 4)
                dve.tensor_tensor(ln_split[rows, 2 * H:3 * H], ln_r[rows, :], ln_split[rows, H:2 * H],
                                  ALU.subtract).then_inc(ln_vec, 1)

            def four_steps(o):
                for r in range(4):
                    rank(4 * o + r, r % 2, 2 * o + r // 2)
                layernorm(o)

            dve.wait_ge(ran, 4)
            four_steps(0)
            with dve.Fori(1, ROUNDS) as o:
                four_steps(o)
            for t in range(ROUNDS, LN_TILES):
                layernorm(t)

            dve.wait_ge(table_in, 16)
            dve.tensor_copy(key_i[:, :], tab[:, :, 0]).then_inc(unpacked_v, 1)
            dve.wait_ge(unpacked_v, 1)
            dve.tensor_single_scalar(dst_part[:, :], key_i[:, :], 8, ALU.arith_shift_right).then_inc(unpacked_v, 1)
            dve.tensor_single_scalar(node_part[:, :], key_i[:, :], KEY - 1, ALU.bitwise_and
                                     ).then_inc(unpacked_v, 1)
            dve.wait_ge(unpacked_a, 2)
            dve.tensor_tensor(a_rest[:, :], a_all[:, :], parts[:, :, 0], ALU.subtract).then_inc(unpacked_v, 1)
            dve.wait_ge(unpacked_v, 4)
            dve.tensor_copy(local[:, :], node_part[:, :]).then_inc(unpacked_v, 1)
            dve.wait_ge(unpacked_a, 3)
            dve.tensor_tensor(third[:, :], a_rest[:, :], parts[:, :, 1], ALU.subtract).then_inc(unpacked_v, 1)
            dve.wait_ge(unpacked_v, 6)
            dve.wait_ge(unpacked_a, 6)
            dve.memset(sums[:, 0:early_end // 2], 0.0).then_inc(cleared, 1)

            for l in range(LAYERS):
                dve.wait_ge(weights_in, 16 * W_DMAS * (l + 1))
                done = 19 * l
                rows_of = ((s_row, w_row), (s_col[:, :], w_col[:, :]))
                for s_, w_ in rows_of:
                    dve.tensor_scalar(s_, w_, 0.0, 2.0, ALU.is_ge, ALU.mult).then_inc(prep_v, 1)
                dve.wait_ge(prep_v, done + 2)
                for s_, w_ in rows_of:
                    dve.tensor_scalar(s_, s_, 1.0, None, ALU.subtract).then_inc(prep_v, 1)
                dve.wait_ge(prep_v, done + 4)
                dve.tensor_tensor(m_row, w_row, s_row, ALU.mult).then_inc(prep_v, 1)
                dve.tensor_tensor(b_row, b_row, s_row, ALU.mult).then_inc(prep_v, 1)
                dve.scalar_tensor_tensor(wh_col[:, :], w_col[:, :], 0.5, s_col[:, :], ALU.mult, ALU.mult
                                         ).then_inc(prep_v, 1)
                dve.scalar_tensor_tensor(bh_col[:, :], b_col[:, :], 0.5, s_col[:, :], ALU.mult, ALU.mult
                                         ).then_inc(prep_v, 1)
                dve.wait_ge(prep_v, done + 8)
                dve.tensor_scalar(m_row, m_row, TINY, None, ALU.max).then_inc(prep_v, 1)
                dve.wait_ge(prep_v, done + 9)
                dve.reciprocal(m_row, m_row).then_inc(prep_v, 1)
                dve.wait_ge(prep_v, done + 10)
                dve.scalar_tensor_tensor(thresh[:, :], b_row, -1.0, m_row, ALU.mult, ALU.mult).then_inc(prep_v, 1)
                dve.memset(d_cols[:, 2:4, 1:2], 0.0).then_inc(prep_v, 1)
                for c in range(HC):
                    dve.tensor_scalar(d_cols[:, c, 0:1], b_col[:, c:c + 1], 0.5, None, ALU.mult
                                      ).then_inc(prep_v, 1)
                    dve.tensor_copy(d_cols[:, 2 + c, 0:1], eb2_col[:, c:c + 1]).then_inc(prep_v, 1)
                    dve.tensor_scalar(d_cols[:, c, 1:2], w_col[:, c:c + 1], 0.5, None, ALU.mult
                                      ).then_inc(prep_v, 1)
                dve.wait_ge(ew2_turned, l + 1)
                dve.tensor_copy(ew2_T[:, :, :].rearrange("p c n -> p (c n)"), ps[0][:, 0:HC * H]
                                ).then_inc(ew2_kept, 1)
                dve.wait_ge(we_summed, l + 1)
                dve.tensor_copy(we[:, :, :].rearrange("p c n -> p (c n)"), ps[1][:, 0:HC * H]).then_inc(we_kept, 1)
                dve.wait_ge(wd_summed, l + 1)
                dve.tensor_copy(wd[:, :], ps[0][0:2, 512:512 + H]).then_inc(prep_v, 1)
                dve.wait_ge(prep_v, done + 19)
                dve.wait_ge(we_kept, l + 1)
                dve.sem_inc(prepared, 1)

                first = l * GROUPS
                dve.wait_ge(cleared, 3)
                ge(dve, emptied, l * PAIRS)

                def nodes(k, g):
                    ge(dve, group_done, first + k - 1)
                    ge(dve, thirds_ready, first + k - 1)
                    for j in range(2):
                        dve.tensor_scalar(hots[:, g % 2, j, 0:P], iota_b[:, :], local[:, bass.ds(2 * k + j, 1)],
                                          None, ALU.is_equal).then_inc(nodes_ready, 1)

                def products(k, g):
                    of = hots[:, g % 2, :, :].rearrange("p j (q n) -> p j q n", q=4)
                    a = parts[:, bass.ds(2 * k, 2), :].rearrange("p j (q n) -> p j q n", n=1)
                    dve.wait_ge(nodes_ready, 2 * (first + k + 1))
                    for j in range(2):
                        op = dve.tensor_tensor(of[:, j, 1:3, :], of[:, j, 0:1, :].broadcast_to([P, 2, P]),
                                               a[:, j, :, :].broadcast_to([P, 2, P]), ALU.mult)
                    op.then_inc(hots_ready, 1)

                def add(k, g):
                    at = dve.value_load(group_block[0:1, bass.ds(k, 1)], min_val=0, max_val=BLOCKS - 1)
                    n = BCOLS if l == 0 else DCOL
                    ge(dve, added, first + k)
                    dve.wait_ge(group_done, first + k + 1)
                    dve.tensor_tensor(block_sums(at, 0, n), block_sums(at, 0, n), ps[g % 2][:, 0:n], ALU.add
                                      ).then_inc(added, 1)

                def body(i, add_first=True, gs=range(4)):
                    for g in range(4):
                        if g in gs:
                            nodes(4 * i + g + 1, g + 1)
                        if g or add_first:
                            add(4 * i + g - 1, g + 1)
                        if g in gs:
                            products(4 * i + g + 1, g + 1)

                nodes(0, 0)
                products(0, 0)
                body(0, False)
                with dve.Fori(1, PASSES - 1) as i:
                    body(i)
                body(PASSES - 1, gs=range(3))
                add(GROUPS - 1, 1)

                mlp_first = l * PAIRS
                last = l == LAYERS - 1
                dve.wait_ge(added, (l + 1) * GROUPS)

                def mlp(q, i, turn, lead, main, trail):
                    if lead:
                        f = mlp_first + q + 1
                        n = blocks_of(q + 1)
                        ge(dve, turned, f - 1)
                        dve.tensor_copy(d_in[:, 1 - i, 0:n, :], pair_sums(q + 1, DCOL, 2)).then_inc(d_taken, 1)
                        for c in range(HC):
                            of_a = pair_sums(q + 1, 2 * c * P + P, P)
                            dve.tensor_scalar(of_a, of_a, wh_col[:, c:c + 1], None, ALU.mult).then_inc(scaled, 1)
                        dve.wait_ge(scaled, HC * (f + 1))
                        for c in range(HC):
                            of_1 = pair_sums(q + 1, 2 * c * P, P)
                            dve.scalar_tensor_tensor(of_1, of_1, bh_col[:, c:c + 1],
                                                     pair_sums(q + 1, 2 * c * P + P, P), ALU.mult, ALU.add
                                                     ).then_inc(rel_ready, 1)
                        dve.wait_ge(turned, f + 1)
                        ge(dve, hid_summed, f - 1)
                        dve.tensor_copy(d_T[:, 1 - i, 0:n * P], ps_d[1 - i][0:2, 0:n * P]).then_inc(dT_ready, 1)
                    if trail:
                        f = mlp_first + q - 1
                        n = blocks_of(q - 1)
                        z = z_out[1 - i][:, 0:n, :]
                        dve.wait_ge(out_summed, f + 1)
                        if last:
                            dve.wait_ge(x_added, q)
                        else:
                            dve.wait_ge(bias_added, f + 1)
                        dve.tensor_tensor(z, ps_out[1 - i][:, 0:n * H].rearrange("p (j n) -> p j n", n=H), z, ALU.add
                                          ).then_inc(z_ready, 1)
                        if not last:
                            dve.tensor_copy(pair_sums(q - 1, 0, DCOL),
                                            zero_col[:, :].rearrange("p (j n) -> p j n", j=1)
                                            .broadcast_to([P, n, DCOL])).then_inc(emptied, 1)
                            dve.wait_ge(hi_ready, f + 1)
                            dve.tensor_tensor(residue[:, 0:n, :], z, z_split[1 - i][:, 0:n, 0:H], ALU.subtract
                                              ).then_inc(res_ready, 1)
                            dve.wait_ge(mid_ready, f + 1)
                            dve.wait_ge(res_ready, f + 1)
                            dve.tensor_tensor(z_split[1 - i][:, 0:n, 2 * H:3 * H], residue[:, 0:n, :],
                                              z_split[1 - i][:, 0:n, H:2 * H], ALU.subtract).then_inc(lo_ready, 1)

                over_pairs(dve, mlp)

        @block.scalar
        def _(act):
            def records(s, h, i):
                ge(act, scattered[h], STEP * 16 * i)
                hold(act)
                act.activation(rec_now[:, h, :, 0], key_f[:, bass.ds(s * STEP, STEP)], ACT.Copy)
                act.activation(rec_now[:, h, :, 1], a_e[:, bass.ds(s * STEP, STEP)], ACT.Copy
                               ).then_inc(recs_ready, 1)

            def layernorm(t):
                rows = slice(0, LN_ROWS)
                act.wait_ge(ln_vec, 6 * t + 2)
                act.activation(ln_std[rows, :], ln_mv[rows, 1:2], ACT.Sqrt, bias=eps_col[rows, :]
                               ).then_inc(ln_act, 1)
                act.wait_ge(ln_vec, 6 * t + 4)
                ge(act, ln_out, 32 * t)
                act.activation(ln_z[rows, :], ln_y[rows, :], ACT.Relu).then_inc(ln_act, 1)
                act.activation(ln_split[rows, 0:H], ln_y[rows, :], ACT.Relu).then_inc(ln_act, 1)
                act.wait_ge(ln_vec, 6 * t + 5)
                act.activation(ln_split[rows, H:2 * H], ln_r[rows, :], ACT.Copy).then_inc(ln_act, 1)

            def four_steps(o):
                for r in range(4):
                    records(4 * o + r, r % 2, 2 * o + r // 2)
                layernorm(o)

            act.wait_ge(keyed, 5)
            act.wait_ge(table_filled, 32)
            four_steps(0)
            with act.Fori(1, ROUNDS) as o:
                four_steps(o)
            for t in range(ROUNDS, LN_TILES):
                layernorm(t)

            act.wait_ge(table_in, 16)
            act.activation(a_all[:, :], tab[:, :, 1], ACT.Copy).then_inc(unpacked_a, 1)
            act.activation(parts[:, :, 0], tab[:, :, 1], ACT.Copy).then_inc(unpacked_a, 1)
            act.wait_ge(unpacked_v, 4)
            act.activation(parts[:, :, 1], a_rest[:, :], ACT.Copy).then_inc(unpacked_a, 1)
            act.wait_ge(unpacked_v, 3)
            act.activation(dst_all[:, :], dst_part[:, :], ACT.Copy).then_inc(unpacked_a, 1)
            act.wait_ge(unpacked_a, 4)
            act.sem_inc(unpacked_a, 2)

            for l in range(LAYERS):
                first = l * GROUPS
                act.wait_ge(prepared, l + 1)

                def stage(k, g, i):
                    ge(act, landed[g], 32 * (l * PASSES + i))
                    hold(act)
                    act.activation(idx_now[:, g, :], dst_all[:, bass.ds(2 * k, 2)], ACT.Copy).then_inc(staged, 1)

                def thirds(k, g):
                    act.wait_ge(nodes_ready, 2 * (first + k + 1))
                    hold(act)
                    for j in range(2):
                        op = act.activation(hots[:, g % 2, j, 3 * P:4 * P], hots[:, g % 2, j, 0:P], ACT.Copy,
                                            scale=third[:, bass.ds(2 * k + j, 1)])
                    op.then_inc(thirds_ready, 1)

                def sign_rows(k, g):
                    ge(act, group_done, first + k - 1)
                    hold(act)
                    for j in range(2):
                        op = act.activation(signs[:, g % 2, j, :], thresh[:, :], ACT.Sign,
                                            bias=a_all[:, bass.ds(2 * k + j, 1)], scale=-1.0)
                    op.then_inc(signs_ready, 1)

                for g in range(4):
                    stage(g, g, 0)
                for g in range(4):
                    sign_rows(g, g)
                    thirds(g, g)
                    stage(4 + g, g, 1)
                with act.Fori(1, PASSES - 1) as i:
                    for g in range(4):
                        sign_rows(4 * i + g, g)
                        thirds(4 * i + g, g)
                        stage(4 * i + 4 + g, g, i + 1)
                for g in range(4):
                    sign_rows(GROUPS - 4 + g, g)
                    thirds(GROUPS - 4 + g, g)

                mlp_first = l * PAIRS
                last = l == LAYERS - 1
                act.wait_ge(added, (l + 1) * GROUPS)

                def mlp(q, i, turn, lead, main, trail):
                    if lead:
                        f = mlp_first + q + 1
                        n = blocks_of(q + 1)
                        act.wait_ge(turned, f + 1)
                        act.wait_ge(rel_ready, HC * (f + 1))
                        hold(act)
                        for c in range(HC):
                            op = act.activation(pair_sums(q + 1, 2 * c * P + P, P),
                                                ps[1 - i][:, c * 2 * P:c * 2 * P + n * P]
                                                .rearrange("p (j n) -> p j n", n=P), ACT.Copy)
                        op.then_inc(zT_ready, 1)
                    if main:
                        n = blocks_of(q)
                        act.wait_ge(hid_summed, mlp_first + q + 1)
                        ge(act, out_summed, mlp_first + q - 1)
                        for c in range(HC):
                            half = slice(c * 2 * P, c * 2 * P + n * P)
                            op = act.activation(hid[i][:, half], ps[i][:, 4 * P:8 * P][:, half], ACT.Relu,
                                                bias=nb1_col[:, c:c + 1])
                        op.then_inc(hid_ready, 1)
                    if trail and not last:
                        f = mlp_first + q - 1
                        n = blocks_of(q - 1)
                        act.wait_ge(z_ready, f + 1)
                        ge(act, stored[1 - i], 32 * (l * fills[1 - i] + turn - 1))
                        act.activation(z_split[1 - i][:, 0:n, 0:H], z_out[1 - i][:, 0:n, :], ACT.Copy
                                       ).then_inc(hi_ready, 1)
                        act.wait_ge(res_ready, f + 1)
                        act.activation(z_split[1 - i][:, 0:n, H:2 * H], residue[:, 0:n, :], ACT.Copy
                                       ).then_inc(mid_ready, 1)

                over_pairs(act, mlp)

        @block.tensor
        def _(pe):
            pe.wait_ge(consts, 9)
            pe.wait_ge(counted, BUCKETS)
            pe.matmul(ps[0][:, 0:BUCKETS], later[:, :], counts[:, :], start=True, stop=True).then_inc(totals, 1)
            pe.matmul(ps[0][0:BUCKETS, 512:513], counts[:, :], ones[:, 0:1], start=True, stop=True
                      ).then_inc(totals, 1)
            pe.wait_ge(quot, 4)
            pe.matmul(ps[1][:, 0:BUCKETS], quot_rows[0:BUCKETS, :], later[0:BUCKETS, 0:BUCKETS],
                      start=True, stop=True).then_inc(bases, 1)
            pe.matmul(ps[1][0:BUCKETS, 512:513], later[0:BUCKETS, 0:BUCKETS], quot_f[0:BUCKETS, :],
                      start=True, stop=True).then_inc(bases, 1)
            pe.wait_ge(starts, 1)
            for n in range(2):
                op = pe.matmul(ps[n][0:1, 0:GROUPS // 2], ones[0:BLOCKS, 0:1],
                               started[0:BLOCKS, n * GROUPS // 2:(n + 1) * GROUPS // 2], start=True, stop=True)
            op.then_inc(grouped, 1)

            for l in range(LAYERS):
                pe.wait_ge(blocks_known, 2)
                pe.wait_ge(weights_in, 16 * W_DMAS * (l + 1))
                for m in range(HC):
                    for c in range(HC):
                        op = pe.transpose(ps[0][:, m * H + c * P:m * H + (c + 1) * P],
                                          ew2_in[:, c, m * P:(m + 1) * P], ident[:, :])
                op.then_inc(ew2_turned, 1)
                pe.wait_ge(ew2_kept, l + 1)
                for c in range(HC):
                    for m in range(HC):
                        op = pe.matmul(ps[1][:, c * H:(c + 1) * H], ew2_T[:, m, c * P:(c + 1) * P], wa[:, m, :],
                                       start=(m == 0), stop=(m == HC - 1))
                op.then_inc(we_summed, 1)
                pe.wait_ge(we_kept, l + 1)
                pe.wait_ge(prep_v, 19 * l + 18)
                for c in range(HC):
                    pe.matmul(ps[0][0:2, 512:512 + H], d_cols[:, c, :], we[:, c, :], start=(c == 0), stop=False)
                for c in range(HC):
                    op = pe.matmul(ps[0][0:2, 512:512 + H], d_cols[:, 2 + c, :], wa[:, c, :], start=False,
                                   stop=(c == HC - 1))
                op.then_inc(wd_summed, 1)
                pe.wait_ge(prepared, l + 1)

                first = l * GROUPS

                def group(k, g, i):
                    pe.wait_ge(hots_ready, first + k + 1)
                    pe.wait_ge(thirds_ready, first + k + 1)
                    pe.wait_ge(signs_ready, first + k + 1)
                    ge(pe, added, first + k - 1)
                    acc = ps[g % 2]
                    for j in range(2):
                        hot_j = hots[:, g % 2, j, :]
                        for c in range(HC):
                            sg = signs[:, g % 2, j, c * P:(c + 1) * P]
                            o = 2 * c * P
                            pe.matmul(acc[:, o:o + 2 * P], sg, hot_j[:, 0:2 * P],
                                      start=(j == 0 and c == 0), stop=False, skip_group_check=True)
                            for q in (2, 3):
                                pe.matmul(acc[:, o + P:o + 2 * P], sg, hot_j[:, q * P:(q + 1) * P],
                                          start=False, stop=(j == 1 and q == 3), skip_group_check=True)
                    pe.wait_ge(landed[g], 32 * (l * PASSES + i + 1))
                    for j in range(2):
                        hot_j = hots[:, g % 2, j, :]
                        for c in range(HC):
                            for q in range(3):
                                op = pe.matmul(acc[:, XCOL + c * P:XCOL + (c + 1) * P],
                                               gath[:, g, j, q * H + c * P:q * H + (c + 1) * P], hot_j[:, 0:P],
                                               start=(j == 0 and c == 0 and q == 0),
                                               stop=(j == 1 and q == 2), skip_group_check=True)
                        if l == 0:
                            for q in range(4):
                                o = DCOL + min(q, 1)
                                op = pe.matmul(acc[:, o:o + 1], hot_j[:, q * P:(q + 1) * P], ones_b[:, :],
                                               start=False, stop=(j == 1 and q in (0, 3)), skip_group_check=True)
                    op.then_inc(group_done, 1)

                for g in range(4):
                    group(g, g, 0)
                with pe.Fori(1, PASSES) as i:
                    for g in range(4):
                        group(4 * i + g, g, i)

                mlp_first = l * PAIRS
                pe.wait_ge(added, (l + 1) * GROUPS)

                def mlp(q, i, turn, lead, main, trail):
                    if lead:
                        f = mlp_first + q + 1
                        n = blocks_of(q + 1)
                        pe.wait_ge(z_loaded[1 - i], 16 * (l * fills[1 - i] + turn + 1))
                        pe.wait_ge(d_taken, f + 1)
                        ge(pe, zT_ready, f - 1)
                        ge(pe, dT_ready, f - 1)
                        for j in range(n):
                            for c in range(HC):
                                o = (2 * c + j) * P
                                pe.transpose(ps[1 - i][:, o:o + P], z_in[1 - i][:, j, c * P:(c + 1) * P],
                                             ident[:, :])
                            op = pe.transpose(ps_d[1 - i][0:2, j * P:(j + 1) * P], d_in[:, 1 - i, j, :], ident[:, :])
                        op.then_inc(turned, 1)
                    if main:
                        f = mlp_first + q
                        n = blocks_of(q)
                        pe.wait_ge(zT_ready, f + 1)
                        pe.wait_ge(dT_ready, f + 1)
                        ge(pe, hid_ready, f - 1)
                        for h in range(HC):
                            fs = slice(h * P, (h + 1) * P)
                            to = ps[i][:, (4 + 2 * h) * P:(4 + 2 * h + n) * P]
                            for c in range(HC):
                                pe.matmul(to, wa[:, c, fs], pair_sums(q, XCOL + c * P, P), start=(c == 0),
                                          stop=False)
                                pe.matmul(to, we[:, c, fs], pair_sums(q, 2 * c * P, P), start=False, stop=False)
                                pe.matmul(to, wx[:, c, fs], pair_sums(q, 2 * c * P + P, P), start=False, stop=False)
                            op = pe.matmul(to, wd[:, fs], d_T[:, i, 0:n * P], start=False, stop=True)
                        op.then_inc(hid_summed, 1)
                    if trail:
                        f = mlp_first + q - 1
                        pe.wait_ge(hid_ready, f + 1)
                        ge(pe, z_ready, f - 1)
                        for j in range(blocks_of(q - 1)):
                            for c in range(HC):
                                o = (2 * c + j) * P
                                op = pe.matmul(ps_out[1 - i][:, j * H:(j + 1) * H], hid[1 - i][:, o:o + P], w2[:, c, :],
                                               start=(c == 0), stop=(c == HC - 1))
                        op.then_inc(out_summed, 1)

                over_pairs(pe, mlp)


_LAYER = ("eW1", "eb1", "eW2", "eb2", "nW1", "nb1", "nW2", "nb2")


def kernel(**inputs):
    import numpy as _np
    import concourse.bacc as _bacc
    from concourse import mybir as _mybir
    from concourse.bass_utils import run_bass_kernel_spmd as _run

    nc = _bacc.Bacc("TRN2", target_bir_lowering=False, num_devices=1)
    arrays = {}

    def given(name):
        a = _np.ascontiguousarray(inputs[name])
        arrays[f"in_{name}"] = a
        return nc.dram_tensor(f"in_{name}", a.shape, _mybir.dt.from_np(a.dtype), kind="ExternalInput").ap()

    edges = [given(name) for name in ("x", "src", "dst", "edge_weight1")]
    weights = [[given(f"L0_gnn_l{l}_{name}") for l in range(LAYERS)] for name in _LAYER]
    out = nc.dram_tensor("out_0", (N_NODES, H), _mybir.dt.float32, kind="ExternalOutput").ap()
    gnn(nc, *edges, *weights, out)
    r = _run(nc, [arrays], core_ids=[0])
    return r.results[0]["out_0"]
```

```python
from contextlib import ExitStack

import concourse.bass as bass
from concourse import mybir

F32 = mybir.dt.float32
BF16 = mybir.dt.bfloat16
I32 = mybir.dt.int32
U32 = mybir.dt.uint32
U16 = mybir.dt.uint16
U8 = mybir.dt.uint8
I16 = mybir.dt.int16
ALU = mybir.AluOpType
ACT = mybir.ActivationFunctionType
AXX = mybir.AxisListType.X

P = 128
N_NODES = 6250
N_EDGES = 200000
H = 256
HC = H // P
LAYERS = 2
EPS = 1e-5
TINY = 1e-30

BLOCKS = -(-N_NODES // P)
BUCKETS = BLOCKS + 1
GROUP = 2 * P
GROUPS = -(-(N_EDGES // GROUP + BLOCKS) // 4) * 4
TILES = 2 * GROUPS
PASSES = GROUPS // 4

STEP = 8
ECOLS = -(-N_EDGES // (P * 4 * STEP)) * 4 * STEP
STEPS = ECOLS // STEP
ROUNDS = STEPS // 4
FULL_P = N_EDGES // ECOLS
LAST_C = N_EDGES - FULL_P * ECOLS
TCOLS = TILES + -(-(P * ECOLS - N_EDGES) // P)
FILL_REPS = 10
FILL_COLS = TCOLS // FILL_REPS
KEY = 256
NO_NODE = P
LN_ROWS = 125
LN_TILES = N_NODES // LN_ROWS
LAST_ROWS = N_NODES - (BLOCKS - 1) * P

XCOL = HC * 2 * P
DCOL = XCOL + HC * P
BCOLS = DCOL + 2
PAIRS = (BLOCKS + 1) // 2
assert PAIRS % 2 == 1
ACT_COUNTS = BUCKETS * 5 // 8
OPS = 14


def ge(eng, sem, value):
    if not (isinstance(value, int) and value <= 0):
        eng.wait_ge(sem, value)


def hold(eng):
    eng.nop(nofuse=True)


def over_pairs(eng, step):
    step(-1, 1, 0, True, False, False)
    step(0, 0, 0, True, True, False)
    step(1, 1, 1, True, True, True)
    step(2, 0, 1, True, True, True)
    with eng.Fori(0, (PAIRS - 7) // 2) as n:
        step(2 * n + 3, 1, n + 2, True, True, True)
        step(2 * n + 4, 0, n + 2, True, True, True)
    for q in range(PAIRS - 4, PAIRS):
        step(q, q % 2, (q + 1) // 2, q + 1 < PAIRS, True, True)
    step(PAIRS, 1, (PAIRS + 1) // 2, False, False, True)


def blocks_of(q):
    return BLOCKS - 2 * q if isinstance(q, int) and q == PAIRS - 1 else 2


def gnn(nc, x, src, dst, ew, eW1, eb1, eW2, eb2, nW1, nb1, nW2, nb2, out):
    table = nc.dram_tensor("sorted_edges", [P * TCOLS, 2], F32, kind="Internal").ap()
    z_rows = nc.dram_tensor("z_rows", [BLOCKS * P, H], F32, kind="Internal").ap()
    split_rows = [nc.dram_tensor(f"split_rows{l}", [rows, 3 * H], BF16, kind="Internal").ap()
                  for l, rows in enumerate((N_NODES, BLOCKS * P))]
    p_cols = nc.dram_tensor("p_cols", [H, BLOCKS * P], F32, kind="Internal").ap()
    we_rows = nc.dram_tensor("we_rows", [LAYERS, H, H], F32, kind="Internal").ap()
    wd_rows = nc.dram_tensor("wd_rows", [LAYERS, 2, H], F32, kind="Internal").ap()
    with ExitStack() as ctx:
        def sb(name, shape, dt):
            return ctx.enter_context(nc.sbuf_tensor(name, shape, dt))

        def sem(name):
            return ctx.enter_context(nc.semaphore(name))

        sums = sb("sums", [P, BLOCKS * BCOLS], F32)
        dst_all = sb("dst_all", [P, TILES], U16)
        a_all = sb("a_all", [P, TILES], F32)
        parts = sb("parts", [P, TILES, 2], BF16)
        third = sb("third", [P, TILES], F32)
        local = sb("local", [P, TILES], U8)
        work = sb("work", [P, 7424], F32)
        later_thresh = sb("later_thresh", [P, H], F32)
        wd = sb("wd", [2, H], F32)

        def column(name):
            return [sb(f"{name}{l}", [P, HC], F32)[:, :] for l in range(LAYERS)]

        w_col, b_col, eb2_col, nb1_col = map(column, "w_col b_col eb2_col nb1_col".split())
        s_col = column("s_col")
        wh_col = column("wh_col")
        bh_col = column("bh_col")
        iota_b = sb("iota_b", [P, P], BF16)
        ident = sb("ident", [P, P], F32)
        d_in = sb("d_in", [P, 2, 2, 2], F32)
        zero_col = sb("zero_col", [P, 1], F32)
        eps_col = sb("eps_col", [P, 1], F32)
        ones_b = sb("ones_b", [P, 1], BF16)
        d_T = sb("d_T", [2, 2, 2 * P], F32)
        group_block = sb("group_block", [1, GROUPS], I16)
        idx_now = sb("idx_now", [P, 4, 2], U32)

        gath = work[:, 0:3072].bitcast(BF16).rearrange("p (g j n) -> p g j n", g=4, j=2)
        hots = work[:, 3072:5120].bitcast(BF16).rearrange("p (g j n) -> p g j n", g=4, j=2)
        signs = work[:, 5120:6144].bitcast(BF16).rearrange("p (g j n) -> p g j n", g=4, j=2)

        def matrix(start):
            return work[:, start:start + HC * H].rearrange("p (c n) -> p c n", c=HC)

        PREP = 13 * H
        ew2_in, ew2_T, wa_in, we_new = ([matrix(PREP * l + HC * H * k) for l in range(LAYERS)] for k in range(4))
        w_row, b_row, s_row, m_row = ([work[:, PREP * l + H * k:PREP * l + H * k + H] for l in range(LAYERS)]
                                      for k in range(8, 12))
        d_cols = [work[:, PREP * l + 12 * H:PREP * l + 12 * H + 8].rearrange("p (c n) -> p c n", c=4)
                  for l in range(LAYERS)]
        wd_new = [work[0:2, PREP * l + 12 * H:PREP * l + 13 * H] for l in range(LAYERS)]
        thresh = [work[:, 26 * H:27 * H], later_thresh[:, :]]

        def two(start, n):
            return [work[:, start + n * i:start + n * i + n] for i in range(2)]

        def by_block(v):
            return v.rearrange("p (j n) -> p j n", j=2)

        z_in = [by_block(v) for v in two(0, 2 * H)]
        z_out = [by_block(v) for v in two(4 * H, 2 * H)]
        hid = two(8 * H, 2 * H)
        z_split = [by_block(v.bitcast(BF16)) for v in two(12 * H, 3 * H)]
        x_in = [by_block(v) for v in two(12 * H, 2 * H)]
        wa = matrix(20 * H)
        we = matrix(22 * H)
        w2 = matrix(24 * H)
        wx = matrix(24 * H)
        p_in = work[:, 26 * H:27 * H]
        p_T, p_out = (work[:, H * k:H * k + H].rearrange("p (c n) -> p c n", c=HC) for k in (27, 28))
        residue = by_block(work[:, 26 * H:28 * H])
        nb2_row = work[:, 28 * H:29 * H]

        taken = [0]

        def early(n, dt=F32):
            v = sums[:, taken[0]:taken[0] + n]
            taken[0] += n
            return v if dt == F32 else v.bitcast(dt)

        src_i = early(ECOLS, I32)
        dst_i = early(ECOLS, I32)
        a_e = early(ECOLS)
        blk_i = early(ECOLS, I32)
        blk_f = early(ECOLS)
        key_f = early(ECOLS)
        blk_b = early(ECOLS // 2, BF16)
        same = [early(ECOLS // 2, BF16) for _ in range(2)]
        fill = early(2 * FILL_COLS).rearrange("p (c w) -> p c w", w=2)
        iota_i = early(GROUPS, I32)
        iota_f = early(GROUPS)
        started = early(GROUPS)
        later = early(P)
        ones = early(P)
        counts = early(BUCKETS)
        side = early(BUCKETS - ACT_COUNTS + 1)
        under = early(BUCKETS)
        sided_signs = [early(ECOLS // 2, BF16) for _ in range(2)]
        quot_f = early(1)
        quot_i = early(2, I32)
        quot_rows = early(P)
        run = early(STEP * BUCKETS).rearrange("p (j b) -> p j b", j=STEP)
        hot = early(STEP * BUCKETS).rearrange("p (j b) -> p j b", j=STEP)
        prod = early(STEP * BUCKETS).rearrange("p (j b) -> p j b", j=STEP)
        pos_f = early(STEP)
        pos_i = early(STEP, I32)
        pos_p = early(STEP, I32)
        pos_c = early(STEP, I32)
        row_now = early(2 * STEP, U32).rearrange("p (h j) -> p h j", h=2)
        rec_now = early(4 * STEP).rearrange("p (h j w) -> p h j w", h=2, w=2)
        ln_x = early(H)
        ln_y = early(H)
        ln_z = early(H)
        ln_r = early(H)
        ln_split = early(3 * H // 2, BF16)
        ln_T = early(H).rearrange("p (c n) -> p c n", c=HC)
        ln_p = early(H).rearrange("p (c n) -> p c n", c=HC)
        wx_first = early(HC * H).rearrange("p (c n) -> p c n", c=HC)
        ln_stats = early(6)
        ln_mv = early(2)
        ln_std = early(1)
        ln_rstd = early(1)
        early_end = taken[0]
        tab = work[:, 12 * H:12 * H + 2 * TILES].rearrange("p (t w) -> p t w", w=2)
        key_i = sums[:, 0:TILES].bitcast(I32)
        dst_part = sums[:, TILES:2 * TILES].bitcast(I32)
        node_part = sums[:, 2 * TILES:3 * TILES].bitcast(I32)
        a_rest = sums[:, 3 * TILES:4 * TILES]
        unpack_end = 4 * TILES
        assert unpack_end <= early_end and 12 * H + 2 * TILES <= 26 * H

        def acc_of(l, g):
            return ps[g if l == 0 else g % 2]

        def block_sums(b, start, n):
            return sums[:, bass.ds(b * BCOLS + start, n)]

        by_blocks = sums[:, :].rearrange("p (b n) -> p b n", n=BCOLS)

        def pair_sums(q, start, n):
            return by_blocks[:, bass.ds(2 * q, blocks_of(q)), start:start + n]

        ps = [ctx.enter_context(nc.psum_tensor(f"ps{i}", [P, 1024], F32)) for i in range(4)]
        ps_d, ps_out = ([ps[k][:, 512 * i:512 * i + 512] for i in range(2)] for k in (2, 3))

        pads_set, src_in, edges_in, table_filled, consts, consts_v = map(
            sem, "pads_set src_in edges_in table_filled consts consts_v".split())
        keyed, counted, sided, totals, quot, bases, ran, starts, grouped, blocks_known = map(
            sem, "keyed counted sided totals quot bases ran starts grouped blocks_known".split())
        ranked, rows_ready, recs_ready, table_in = map(
            sem, "ranked rows_ready recs_ready table_in".split())
        scattered = [sem("scattered0"), sem("scattered1")]
        ln_in, ln_vec, ln_act, ln_out = map(sem, "ln_in ln_vec ln_act ln_out".split())
        p_turned, p_kept, p_summed, p_ready, p_stored, p_here, pre_ready = map(
            sem, "p_turned p_kept p_summed p_ready p_stored p_here pre_ready".split())
        unpacked_v, unpacked_a, cleared = map(sem, "unpacked_v unpacked_a cleared".split())
        weights_in, prep_v, ew2_turned, ew2_kept, we_summed, we_kept, wd_summed, wd_kept = map(
            sem, "weights_in prep_v ew2_turned ew2_kept we_summed we_kept wd_summed wd_kept".split())
        prep_stored, weights_here = map(sem, "prep_stored weights_here".split())
        staged, nodes_ready, thirds_ready, hots_ready, signs_ready, group_done, added = map(
            sem, "staged nodes_ready thirds_ready hots_ready signs_ready group_done added".split())
        landed = [sem(f"landed{g}") for g in range(4)]
        turned, dT_ready, rel_ready, hid_summed, hid_ready, out_summed = map(
            sem, "turned dT_ready rel_ready hid_summed hid_ready out_summed".split())
        d_taken, scaled, bias_added, z_ready, hi_ready, res_ready, mid_ready, lo_ready = map(
            sem, "d_taken scaled bias_added z_ready hi_ready res_ready mid_ready lo_ready".split())
        x_added, emptied = sem("x_added"), sem("emptied")
        z_loaded, x_loaded, p_loaded, stored = ([sem(f"{n}{i}") for i in range(2)]
                                                for n in ("z_loaded", "x_loaded", "p_loaded", "stored"))
        fills = [(PAIRS + 1) // 2, PAIRS // 2]

        block = ctx.enter_context(nc.Block())
        W_DMAS = 8
        HERE_DMAS = 5
        P_BODIES = 1 + BLOCKS

        def flat(v):
            return v.rearrange("a n -> (a n)")

        def everywhere(v):
            return v.rearrange("(a n) -> a n", a=1).broadcast_to([P, H])

        @block.sync
        def _(sp):
            def edges(dest, v, done):
                sp.dma_start(dest[0:FULL_P, :], v[0:FULL_P * ECOLS].rearrange("(p c) -> p c", c=ECOLS)
                             ).then_inc(done, 16)
                sp.dma_start(dest[FULL_P:FULL_P + 1, 0:LAST_C],
                             v[FULL_P * ECOLS:N_EDGES].rearrange("(p c) -> p c", p=1)).then_inc(done, 16)

            sp.wait_ge(pads_set, 4)
            edges(src_i, src, src_in)
            edges(dst_i, dst, edges_in)
            edges(a_e, ew.rearrange("e w -> (e w)"), edges_in)
            sp.dma_start(table.rearrange("(p r n) w -> p r (n w)", p=P, r=FILL_REPS),
                         fill[:, :, :].rearrange("p (r c) w -> p r (c w)", r=1)
                         .broadcast_to([P, FILL_REPS, 2 * FILL_COLS])).then_inc(table_filled, 16)
            sp.dma_start(z_rows[N_NODES:BLOCKS * P, :], ln_z[0:BLOCKS * P - N_NODES, :]
                         ).then_inc(table_filled, 16)
            sp.dma_start(p_cols.rearrange("(c p) n -> p c n", p=P)[:, :, N_NODES:BLOCKS * P],
                         ln_z[:, 0:HC * (BLOCKS * P - N_NODES)].rearrange("p (c n) -> p c n", c=HC)
                         ).then_inc(table_filled, 16)

            def layernorm(t):
                ge(sp, ln_vec, 6 * t)
                sp.dma_start(ln_x[0:LN_ROWS, :], x[bass.ds(t * LN_ROWS, LN_ROWS), :]).then_inc(ln_in, 16)
                sp.wait_ge(ln_vec, 6 * t + 6)
                sp.dma_start(z_rows[bass.ds(t * LN_ROWS, LN_ROWS), :], ln_z[0:LN_ROWS, :]
                             ).then_inc(ln_out, 16)
                sp.dma_start(split_rows[0][bass.ds(t * LN_ROWS, LN_ROWS), :], ln_split[0:LN_ROWS, :]
                             ).then_inc(ln_out, 16)
                sp.wait_ge(p_ready, t + 1)
                hold(sp)
                sp.dma_start(p_cols.rearrange("(c p) n -> p c n", p=P)[:, :, bass.ds(t * LN_ROWS, LN_ROWS)],
                             ln_p[:, :, 0:LN_ROWS]).then_inc(p_stored, 16)

            for l in range(LAYERS):
                for dest, v in ((w_row[l], flat(eW1[l])), (b_row[l], eb1[l])):
                    sp.dma_start(dest, everywhere(v)).then_inc(weights_in, 16)
                for dest, v in ((w_col[l], flat(eW1[l])), (b_col[l], eb1[l]), (eb2_col[l], eb2[l]),
                                (nb1_col[l], nb1[l])):
                    sp.dma_start(dest, v.rearrange("(c p) -> p c", p=P),
                                 allow_slow_non_contiguous=True).then_inc(weights_in, 16)
                for dest, v in ((wa_in[l], nW1[l][H:2 * H, :]), (ew2_in[l], eW2[l])):
                    sp.dma_start(dest, v.rearrange("(c p) n -> p c n", p=P)).then_inc(weights_in, 16)
            sp.dma_start(wx_first, nW1[0][0:H, :].rearrange("(c p) n -> p c n", p=P)).then_inc(weights_in, 16)
            sp.wait_ge(table_filled, 48)
            layernorm(0)
            layernorm(1)
            for l in range(LAYERS):
                sp.wait_ge(we_kept, l + 1)
                sp.dma_start(we_rows[l].rearrange("(c p) n -> p c n", p=P), we_new[l]).then_inc(prep_stored, 16)
                sp.wait_ge(wd_kept, l + 1)
                sp.dma_start(wd_rows[l], wd_new[l]).then_inc(prep_stored, 16)
            with sp.Fori(2, LN_TILES) as t:
                layernorm(t)
            for h in range(2):
                sp.wait_ge(scattered[h], STEPS // 2 * STEP * 16)
            sp.wait_ge(prep_stored, 32 * LAYERS)
            sp.dma_start(tab, table.rearrange("(p t) w -> p t w", p=P)[:, 0:TILES, :]).then_inc(table_in, 16)

            for l in range(LAYERS):
                first = l * PAIRS
                last = l == LAYERS - 1
                if l > 0:
                    sp.dma_start(wx, nW1[l][0:H, :].rearrange("(c p) n -> p c n", p=P)).then_inc(p_here, 16)
                    with sp.Fori(0, BLOCKS) as t:
                        sp.wait_ge(p_turned, LN_TILES + t)
                        hold(sp)
                        sp.dma_start(p_in, z_rows[bass.ds(t * P, P), :]).then_inc(p_here, 16)
                        sp.wait_ge(p_ready, LN_TILES + t + 1)
                        hold(sp)
                        sp.dma_start(p_cols.rearrange("(c p) n -> p c n", p=P)[:, :, bass.ds(t * P, P)], p_out
                                     ).then_inc(p_stored, 16)
                sp.wait_ge(added, (l + 1) * GROUPS)

                def rows(dram, q):
                    n = blocks_of(q)
                    return dram[bass.ds(q * 2 * P, n * P), :].rearrange("(j p) n -> p j n", p=P), n

                def load_rows(q, i):
                    ge(sp, bias_added, first + q - 1)
                    v, n = rows(z_rows, q)
                    sp.dma_start(z_in[i][:, 0:n, :], v).then_inc(z_loaded[i], 16)
                    if last:
                        ge(sp, x_added, q - 1)
                        if n == 1:
                            sp.dma_start(x_in[i][0:LAST_ROWS, 0, :], x[N_NODES - LAST_ROWS:N_NODES, :]
                                         ).then_inc(x_loaded[i], 16)
                        else:
                            sp.dma_start(x_in[i][:, :, :], rows(x, q)[0]).then_inc(x_loaded[i], 16)

                def load_products(q, i):
                    ge(sp, out_summed, first + q - 1)
                    hold(sp)
                    n = blocks_of(q)
                    sp.dma_start(hid[i].rearrange("p (c n) -> p c n", c=HC)[:, :, 0:n * P],
                                 p_cols.rearrange("(c p) n -> p c n", p=P)[:, :, bass.ds(q * 2 * P, n * P)]
                                 ).then_inc(p_loaded[i], 16)

                def mlp_io(q, i, turn, lead, main, trail):
                    if lead:
                        load_products(q + 1, 1 - i)
                    if not isinstance(q, int) or q + 2 < PAIRS:
                        load_rows(q + 2, i)
                    if trail:
                        if last:
                            ge(sp, z_ready, first + q)
                            if blocks_of(q - 1) == 1:
                                sp.dma_start(out[N_NODES - LAST_ROWS:N_NODES, :], z_out[1 - i][0:LAST_ROWS, 0, :]
                                             ).then_inc(stored[1 - i], 16)
                            else:
                                sp.dma_start(rows(out, q - 1)[0], z_out[1 - i][:, :, :]
                                             ).then_inc(stored[1 - i], 16)
                        else:
                            ge(sp, lo_ready, q)
                            v, n = rows(z_rows, q - 1)
                            sp.dma_start(v, z_out[1 - i][:, 0:n, :]).then_inc(stored[1 - i], 16)
                            sp.dma_start(rows(split_rows[l + 1], q - 1)[0], z_split[1 - i][:, 0:n, :]
                                         ).then_inc(stored[1 - i], 16)

                load_rows(0, 0)
                sp.wait_ge(p_stored, 16 * (LN_TILES + l * BLOCKS))
                sp.dma_start(nb2_row, everywhere(nb2[l])).then_inc(weights_here, 16)
                sp.dma_start(wd[:, :], wd_rows[l]).then_inc(weights_here, 16)
                for dest, v in ((wa, nW1[l][H:2 * H, :]), (we, we_rows[l]), (w2, nW2[l])):
                    sp.dma_start(dest, v.rearrange("(c p) n -> p c n", p=P)).then_inc(weights_here, 16)
                over_pairs(sp, mlp_io)
                for i in range(2):
                    sp.wait_ge(stored[i], fills[i] * (32 * l + (16 if last else 32)))

        @block.gpsimd
        def _(pool):
            tail = slice(P // 4 * 3, P)
            pool.memset(src_i[tail, LAST_C:ECOLS], BLOCKS * P).then_inc(pads_set, 1)
            pool.memset(dst_i[tail, LAST_C:ECOLS], 0).then_inc(pads_set, 1)
            pool.memset(a_e[tail, LAST_C:ECOLS], 0.0).then_inc(pads_set, 1)
            pool.wait_ge(pads_set, 3)
            pool.memset(fill[:, :, 0:1], float(NO_NODE)).then_inc(consts, 1)
            pool.memset(fill[:, :, 1:2], 0.0).then_inc(consts, 1)
            pool.memset(ln_z[:, :], 0.0).then_inc(consts, 1)
            pool.memset(ones[:, :], 1.0).then_inc(consts, 1)
            pool.memset(zero_col[:, :], 0.0).then_inc(consts, 1)
            pool.memset(eps_col[:, :], EPS).then_inc(consts, 1)
            pool.iota(iota_i[:, :], pattern=[[1, GROUPS]], base=0, channel_multiplier=0).then_inc(consts, 1)
            pool.wait_ge(consts, 7)
            pool.sem_inc(pads_set, 1)
            pool.affine_select(out=later[:, :], in_=ones[:, :], compare_op=ALU.is_gt, fill=0.0, base=0,
                               pattern=[[1, P]], channel_multiplier=-1).then_inc(consts, 1)
            pool.affine_select(out=ident[:, :], in_=ones[:, :], compare_op=ALU.is_equal, fill=0.0, base=0,
                               pattern=[[1, P]], channel_multiplier=-1).then_inc(consts, 1)
            pool.memset(ones_b[:, :], 1.0).then_inc(consts, 1)
            pool.memset(sums[:, early_end:BLOCKS * BCOLS], 0.0).then_inc(cleared, 1)
            pool.wait_ge(table_filled, 48)

            def scatter(s, h):
                pool.wait_ge(rows_ready, s + 1)
                pool.wait_ge(recs_ready, s + 1)
                hold(pool)
                for j in range(STEP):
                    pool.indirect_dma_start(
                        table, bass.IndirectOffsetOnAxis(ap=row_now[:, h, j:j + 1], axis=0),
                        rec_now[:, h, j, :], None).then_inc(scattered[h], 16)

            with pool.Fori(0, STEPS // 2) as i:
                for h in range(2):
                    scatter(2 * i + h, h)

            for l in range(LAYERS):
                first = l * GROUPS
                if l == 0:
                    pool.wait_ge(ln_out, 32 * LN_TILES)
                    pool.wait_ge(p_stored, 16 * LN_TILES)
                    pool.wait_ge(ln_vec, 6 * LN_TILES)
                    pool.wait_ge(ranked, STEPS * OPS)
                    for h in range(2):
                        pool.wait_ge(scattered[h], STEPS // 2 * STEP * 16)
                    pool.memset(sums[:, unpack_end:early_end], 0.0).then_inc(cleared, 1)
                    pool.wait_ge(prep_stored, 32 * LAYERS)
                else:
                    for i in range(2):
                        pool.wait_ge(stored[i], 32 * fills[i] * l)

                def gather(k, g):
                    ge(pool, group_done, first + k - 3)
                    pool.wait_ge(staged, first + k + 1)
                    hold(pool)
                    for j in range(2):
                        pool.indirect_dma_start(
                            gath[:, g, j, :], None, split_rows[l],
                            bass.IndirectOffsetOnAxis(ap=idx_now[:, g, j:j + 1], axis=0)
                        ).then_inc(landed[g], 16)

                for g in range(4):
                    gather(g, g)
                with pool.Fori(1, PASSES) as i:
                    for g in range(4):
                        gather(4 * i + g, g)

                mlp_first = l * PAIRS
                last = l == LAYERS - 1
                pool.wait_ge(added, (l + 1) * GROUPS)
                pool.wait_ge(weights_here, 16 * HERE_DMAS * (l + 1))

                def add_bias(q, i, turn, lead, main, trail):
                    if lead:
                        n = blocks_of(q + 1)
                        to = z_out[1 - i][:, 0:n, :]
                        pool.wait_ge(z_loaded[1 - i], 16 * (l * fills[1 - i] + turn + 1))
                        ge(pool, stored[1 - i], l * fills[1 - i] * 32 + turn * (16 if last else 32))
                        hold(pool)
                        pool.tensor_tensor(to, z_in[1 - i][:, 0:n, :],
                                           nb2_row.rearrange("p (j n) -> p j n", j=1).broadcast_to([P, n, H]),
                                           ALU.add).then_inc(bias_added, 1)
                        if last:
                            pool.wait_ge(bias_added, mlp_first + q + 2)
                            pool.wait_ge(x_loaded[1 - i], 16 * (turn + 1))
                            hold(pool)
                            pool.tensor_tensor(to, to, x_in[1 - i][:, 0:n, :], ALU.add).then_inc(x_added, 1)

                over_pairs(pool, add_bias)

        @block.vector
        def _(dve):
            dve.wait_ge(consts, 9)
            dve.tensor_copy(iota_f[:, :], iota_i[:, :]).then_inc(consts_v, 1)
            dve.tensor_copy(iota_b[:, :], iota_i[:, 0:P]).then_inc(consts_v, 1)
            dve.memset(side[:, BUCKETS - ACT_COUNTS:BUCKETS - ACT_COUNTS + 1], -float(ECOLS)).then_inc(consts_v, 1)
            dve.wait_ge(consts_v, 3)
            dve.tensor_scalar(under[:, :], iota_f[:, 0:BUCKETS], -1.0, 0.5, ALU.mult, ALU.add).then_inc(consts_v, 1)
            dve.wait_ge(src_in, 32)
            dve.tensor_single_scalar(blk_i[:, :], src_i[:, :], 7, ALU.arith_shift_right).then_inc(keyed, 1)
            dve.wait_ge(keyed, 1)
            dve.tensor_copy(blk_b[:, :], blk_i[:, :]).then_inc(keyed, 1)
            dve.tensor_copy(blk_f[:, :], blk_i[:, :]).then_inc(keyed, 1)
            dve.wait_ge(keyed, 3)
            for b in range(ACT_COUNTS):
                ge(dve, counted, b - 1)
                dve.tensor_scalar(same[b % 2], blk_b[:, :], float(b), 0.0, ALU.is_equal, ALU.add,
                                  accum_out=counts[:, b:b + 1]).then_inc(counted, 1)
            n = BUCKETS - ACT_COUNTS
            dve.wait_ge(sided, n)
            dve.tensor_tensor(counts[:, ACT_COUNTS:BUCKETS], side[:, 0:n], side[:, 1:n + 1], ALU.subtract
                              ).then_inc(counted, 1)
            dve.wait_ge(counted, ACT_COUNTS + 1)
            dve.tensor_scalar(counts[:, ACT_COUNTS:BUCKETS], counts[:, ACT_COUNTS:BUCKETS], 0.5, None, ALU.mult
                              ).then_inc(counted, 1)
            dve.wait_ge(edges_in, 64)
            dve.scalar_tensor_tensor(key_f[:, :], dst_i[:, :], float(KEY), src_i[:, :], ALU.mult, ALU.add
                                     ).then_inc(keyed, 1)
            dve.wait_ge(keyed, 4)
            dve.scalar_tensor_tensor(key_f[:, :], blk_f[:, :], float(-P), key_f[:, :], ALU.mult, ALU.add
                                     ).then_inc(keyed, 1)
            dve.wait_ge(totals, 2)
            dve.tensor_scalar(quot_i[0:BUCKETS, 0:1], ps[0][0:BUCKETS, 512:513], float(GROUP - 1), None, ALU.add
                              ).then_inc(quot, 1)
            dve.wait_ge(quot, 1)
            dve.tensor_single_scalar(quot_i[0:BUCKETS, 1:2], quot_i[0:BUCKETS, 0:1], 8, ALU.arith_shift_right
                                     ).then_inc(quot, 1)
            dve.wait_ge(quot, 2)
            dve.tensor_copy(quot_f[0:BUCKETS, :], quot_i[0:BUCKETS, 1:2]).then_inc(quot, 1)
            dve.wait_ge(quot, 3)
            dve.tensor_scalar(quot_rows[0:BUCKETS, :], ones[0:BUCKETS, :], quot_f[0:BUCKETS, 0:1], None, ALU.mult
                              ).then_inc(quot, 1)
            dve.wait_ge(bases, 2)
            dve.tensor_copy(prod[:, 0, :], ps[0][:, 0:BUCKETS]).then_inc(ran, 1)
            dve.wait_ge(ran, 1)
            dve.scalar_tensor_tensor(run[:, 0, 0:BLOCKS], ps[1][:, 0:BLOCKS], float(GROUP), prod[:, 0, 0:BLOCKS],
                                     ALU.mult, ALU.add).then_inc(ran, 1)
            dve.tensor_scalar(run[:, 0, BLOCKS:BUCKETS], prod[:, 0, BLOCKS:BUCKETS], float(GROUPS * GROUP), None,
                              ALU.add).then_inc(ran, 1)
            dve.tensor_copy(quot_f[0:BLOCKS, :], ps[1][0:BLOCKS, 512:513]).then_inc(ran, 1)
            dve.wait_ge(ran, 4)
            dve.tensor_scalar(started[0:BLOCKS, :], iota_f[0:BLOCKS, :], quot_f[0:BLOCKS, 0:1], None, ALU.is_ge
                              ).then_inc(starts, 1)
            dve.wait_ge(grouped, 1)
            for n in range(2):
                dve.tensor_scalar(group_block[:, n * GROUPS // 2:(n + 1) * GROUPS // 2],
                                  ps[n][0:1, 0:GROUPS // 2], -1.0, None, ALU.add).then_inc(blocks_known, 1)

            def rank(s, h, i):
                done = s * OPS
                ge(dve, ranked, done)
                dve.tensor_tensor(hot[:, :, :],
                                  iota_f[:, 0:BUCKETS].rearrange("p (j b) -> p j b", j=1)
                                  .broadcast_to([P, STEP, BUCKETS]),
                                  blk_f[:, bass.ds(s * STEP, STEP)].rearrange("p (j b) -> p j b", b=1)
                                  .broadcast_to([P, STEP, BUCKETS]), ALU.is_equal).then_inc(ranked, 1)
                for j in range(STEP - 1):
                    dve.wait_ge(ranked, done + 1 + j)
                    dve.tensor_tensor(run[:, j + 1, :], run[:, j, :], hot[:, j, :], ALU.add).then_inc(ranked, 1)
                dve.wait_ge(ranked, done + STEP)
                dve.tensor_tensor(prod[:, :, :], run[:, :, :], hot[:, :, :], ALU.mult).then_inc(ranked, 1)
                dve.wait_ge(ranked, done + STEP + 1)
                dve.tensor_reduce(pos_f[:, :], prod[:, :, :], AXX, ALU.add).then_inc(ranked, 1)
                dve.tensor_tensor(run[:, 0, :], run[:, STEP - 1, :], hot[:, STEP - 1, :], ALU.add
                                  ).then_inc(ranked, 1)
                dve.wait_ge(ranked, done + STEP + 3)
                dve.tensor_copy(pos_i[:, :], pos_f[:, :]).then_inc(ranked, 1)
                dve.wait_ge(ranked, done + STEP + 4)
                dve.tensor_single_scalar(pos_p[:, :], pos_i[:, :], P - 1, ALU.bitwise_and).then_inc(ranked, 1)
                dve.tensor_single_scalar(pos_c[:, :], pos_i[:, :], 7, ALU.arith_shift_right).then_inc(ranked, 1)
                dve.wait_ge(ranked, done + STEP + 6)
                ge(dve, scattered[h], STEP * 16 * i)
                dve.scalar_tensor_tensor(row_now[:, h, :], pos_p[:, :], float(TCOLS), pos_c[:, :],
                                         ALU.mult, ALU.add).then_inc(rows_ready, 1)

            def layernorm(t):
                done = 6 * t
                rows = slice(0, LN_ROWS)
                dve.wait_ge(ln_in, 16 * (t + 1))
                dve.bn_stats(ln_stats[rows, :], ln_x[rows, :]).then_inc(ln_vec, 1)
                dve.wait_ge(ln_vec, done + 1)
                hold(dve)
                dve.bn_aggr(ln_mv[rows, :], ln_stats[rows, :]).then_inc(ln_vec, 1)
                dve.wait_ge(ln_act, 4 * t + 1)
                dve.reciprocal(ln_rstd[rows, :], ln_std[rows, :]).then_inc(ln_vec, 1)
                dve.wait_ge(ln_vec, done + 3)
                dve.tensor_scalar(ln_y[rows, :], ln_x[rows, :], ln_mv[rows, 0:1], ln_rstd[rows, 0:1],
                                  ALU.subtract, ALU.mult).then_inc(ln_vec, 1)
                dve.wait_ge(ln_act, 4 * t + 3)
                dve.tensor_tensor(ln_r[rows, :], ln_z[rows, :], ln_split[rows, 0:H], ALU.subtract
                                  ).then_inc(ln_vec, 1)
                dve.wait_ge(ln_vec, done + 5)
                dve.wait_ge(ln_act, 4 * t + 4)
                dve.tensor_tensor(ln_split[rows, 2 * H:3 * H], ln_r[rows, :], ln_split[rows, H:2 * H],
                                  ALU.subtract).then_inc(ln_vec, 1)

            def prepare(l, part):
                if part == 0:
                    dve.wait_ge(weights_in, 16 * (W_DMAS * LAYERS + 1))
                    done = 18 * l
                    rows_of = ((s_row[l], w_row[l]), (s_col[l], w_col[l]))
                    for s_, w_ in rows_of:
                        dve.tensor_scalar(s_, w_, 0.0, 2.0, ALU.is_ge, ALU.mult).then_inc(prep_v, 1)
                    dve.wait_ge(prep_v, done + 2)
                    for s_, w_ in rows_of:
                        dve.tensor_scalar(s_, s_, 1.0, None, ALU.subtract).then_inc(prep_v, 1)
                    dve.wait_ge(prep_v, done + 4)
                    dve.tensor_tensor(m_row[l], w_row[l], s_row[l], ALU.mult).then_inc(prep_v, 1)
                    dve.tensor_tensor(b_row[l], b_row[l], s_row[l], ALU.mult).then_inc(prep_v, 1)
                    dve.scalar_tensor_tensor(wh_col[l], w_col[l], 0.5, s_col[l], ALU.mult, ALU.mult
                                             ).then_inc(prep_v, 1)
                    dve.scalar_tensor_tensor(bh_col[l], b_col[l], 0.5, s_col[l], ALU.mult, ALU.mult
                                             ).then_inc(prep_v, 1)
                    dve.wait_ge(prep_v, done + 8)
                    dve.tensor_scalar(m_row[l], m_row[l], TINY, None, ALU.max).then_inc(prep_v, 1)
                    dve.wait_ge(prep_v, done + 9)
                    dve.reciprocal(m_row[l], m_row[l]).then_inc(prep_v, 1)
                    dve.wait_ge(prep_v, done + 10)
                    dve.scalar_tensor_tensor(thresh[l], b_row[l], -1.0, m_row[l], ALU.mult, ALU.mult
                                             ).then_inc(prep_v, 1)
                    dve.memset(d_cols[l][:, 2:4, 1:2], 0.0).then_inc(prep_v, 1)
                    for c in range(HC):
                        dve.tensor_scalar(d_cols[l][:, c, 0:1], b_col[l][:, c:c + 1], 0.5, None, ALU.mult
                                          ).then_inc(prep_v, 1)
                        dve.tensor_copy(d_cols[l][:, 2 + c, 0:1], eb2_col[l][:, c:c + 1]).then_inc(prep_v, 1)
                        dve.tensor_scalar(d_cols[l][:, c, 1:2], w_col[l][:, c:c + 1], 0.5, None, ALU.mult
                                          ).then_inc(prep_v, 1)
                elif part == 1:
                    dve.wait_ge(ew2_turned, l + 1)
                    dve.tensor_copy(ew2_T[l].rearrange("p c n -> p (c n)"), ps[0][:, 0:HC * H]).then_inc(ew2_kept, 1)
                elif part == 2:
                    dve.wait_ge(we_summed, l + 1)
                    dve.tensor_copy(we_new[l].rearrange("p c n -> p (c n)"), ps[1][:, 0:HC * H]).then_inc(we_kept, 1)
                elif part == 3:
                    dve.wait_ge(wd_summed, l + 1)
                    dve.tensor_copy(wd_new[l], ps[0][0:2, 512:512 + H]).then_inc(wd_kept, 1)

            def four_steps(o, layer=None):
                for r in range(4):
                    rank(4 * o + r, r % 2, 2 * o + r // 2)
                    if layer is not None:
                        prepare(layer, r)
                layernorm(o)

            dve.wait_ge(ran, 4)
            for o in range(LAYERS):
                four_steps(o, layer=o)
            with dve.Fori(LAYERS, ROUNDS) as o:
                four_steps(o)
            for t in range(ROUNDS, LN_TILES):
                layernorm(t)

            dve.wait_ge(table_in, 16)
            dve.tensor_copy(key_i[:, :], tab[:, :, 0]).then_inc(unpacked_v, 1)
            dve.wait_ge(unpacked_v, 1)
            dve.tensor_single_scalar(dst_part[:, :], key_i[:, :], 8, ALU.arith_shift_right).then_inc(unpacked_v, 1)
            dve.tensor_single_scalar(node_part[:, :], key_i[:, :], KEY - 1, ALU.bitwise_and
                                     ).then_inc(unpacked_v, 1)
            dve.wait_ge(unpacked_v, 3)
            dve.tensor_copy(local[:, :], node_part[:, :]).then_inc(unpacked_v, 1)
            dve.wait_ge(unpacked_a, 3)
            dve.tensor_tensor(a_rest[:, :], a_all[:, :], parts[:, :, 0], ALU.subtract).then_inc(unpacked_v, 1)
            dve.wait_ge(unpacked_v, 5)
            dve.memset(sums[:, 0:3 * TILES], 0.0).then_inc(cleared, 1)
            dve.wait_ge(unpacked_a, 4)
            dve.tensor_tensor(third[:, :], a_rest[:, :], parts[:, :, 1], ALU.subtract).then_inc(unpacked_v, 1)
            dve.wait_ge(unpacked_v, 6)
            dve.memset(sums[:, 3 * TILES:unpack_end], 0.0).then_inc(cleared, 1)

            for l in range(LAYERS):
                first = l * GROUPS
                dve.wait_ge(cleared, 4)
                dve.wait_ge(prep_stored, 32 * LAYERS)
                ge(dve, emptied, l * PAIRS)
                if l > 0:
                    for i in range(2):
                        dve.wait_ge(stored[i], 32 * fills[i] * l)

                def nodes(k, g):
                    ge(dve, group_done, first + k - 3)
                    for j in range(2):
                        dve.tensor_scalar(hots[:, g, j, 0:P], iota_b[:, :], local[:, bass.ds(2 * k + j, 1)],
                                          None, ALU.is_equal).then_inc(nodes_ready, 1)

                def products(k, g):
                    of = hots[:, g, :, :].rearrange("p j (q n) -> p j q n", q=4)
                    a = parts[:, bass.ds(2 * k, 2), :].rearrange("p j (q n) -> p j q n", n=1)
                    dve.wait_ge(nodes_ready, 2 * (first + k + 1))
                    for j in range(2):
                        op = dve.tensor_tensor(of[:, j, 1:3, :], of[:, j, 0:1, :].broadcast_to([P, 2, P]),
                                               a[:, j, :, :].broadcast_to([P, 2, P]), ALU.mult)
                    op.then_inc(hots_ready, 1)

                def block_of(k):
                    return dve.value_load(group_block[0:1, bass.ds(k, 1)], min_val=0, max_val=BLOCKS - 1)

                def add(k, g, at):
                    n = BCOLS if l == 0 else DCOL
                    ge(dve, added, first + k)
                    dve.wait_ge(group_done, first + k + 1)
                    dve.tensor_tensor(block_sums(at, 0, n), block_sums(at, 0, n), acc_of(l, g)[:, 0:n], ALU.add
                                      ).then_inc(added, 1)

                def body(i, add_first=True, gs=range(4)):
                    for g in range(4):
                        ahead, behind = (g + 2) % 4, (g + 3) % 4
                        if g or add_first:
                            at = block_of(4 * i + g - 1)
                        if g in gs:
                            nodes(4 * i + g + 2, ahead)
                        if g or add_first:
                            add(4 * i + g - 1, behind, at)
                        if g in gs:
                            products(4 * i + g + 2, ahead)

                for g in range(2):
                    nodes(g, g)
                    products(g, g)
                body(0, False)
                with dve.Fori(1, PASSES - 1) as i:
                    body(i)
                body(PASSES - 1, gs=range(2))
                add(GROUPS - 1, 3, block_of(GROUPS - 1))

                mlp_first = l * PAIRS
                last = l == LAYERS - 1
                dve.wait_ge(added, (l + 1) * GROUPS)

                def take_d(q, i):
                    ge(dve, turned, mlp_first + q - 1)
                    dve.tensor_copy(d_in[:, i, 0:blocks_of(q), :], pair_sums(q, DCOL, 2)).then_inc(d_taken, 1)

                def scale(q):
                    for c in range(HC):
                        of_a = pair_sums(q, 2 * c * P + P, P)
                        dve.tensor_scalar(of_a, of_a, wh_col[l][:, c:c + 1], None, ALU.mult).then_inc(scaled, 1)
                    dve.wait_ge(scaled, HC * (mlp_first + q + 1))
                    for c in range(HC):
                        of_1 = pair_sums(q, 2 * c * P, P)
                        dve.scalar_tensor_tensor(of_1, of_1, bh_col[l][:, c:c + 1],
                                                 pair_sums(q, 2 * c * P + P, P), ALU.mult, ALU.add
                                                 ).then_inc(rel_ready, 1)

                take_d(0, 0)
                take_d(1, 1)
                scale(0)

                def mlp(q, i, turn, lead, main, trail):
                    if lead:
                        f = mlp_first + q + 1
                        n = blocks_of(q + 1)
                        dve.wait_ge(turned, f + 1)
                        ge(dve, hid_summed, f - 1)
                        dve.tensor_copy(d_T[:, 1 - i, 0:n * P], ps_d[1 - i][0:2, 0:n * P]).then_inc(dT_ready, 1)
                    if main and (not isinstance(q, int) or q + 2 < PAIRS):
                        take_d(q + 2, i)
                    if main:
                        n = blocks_of(q)
                        dve.wait_ge(hid_summed, mlp_first + q + 1)
                        dve.wait_ge(p_loaded[i], 16 * (l * fills[i] + turn + 1 - i))
                        h = hid[i].rearrange("p (c n) -> p c n", c=HC)[:, :, 0:n * P]
                        dve.tensor_tensor(h, ps[i][:, 4 * P:8 * P].rearrange("p (c n) -> p c n", c=HC)[:, :, 0:n * P],
                                          h, ALU.add).then_inc(pre_ready, 1)
                    if trail:
                        f = mlp_first + q - 1
                        n = blocks_of(q - 1)
                        z = z_out[1 - i][:, 0:n, :]
                        dve.wait_ge(out_summed, f + 1)
                        if last:
                            dve.wait_ge(x_added, q)
                        else:
                            dve.wait_ge(bias_added, f + 1)
                        dve.tensor_tensor(z, ps_out[1 - i][:, 0:n * H].rearrange("p (j n) -> p j n", n=H), z, ALU.add
                                          ).then_inc(z_ready, 1)
                    if not isinstance(q, int) or q + 2 < PAIRS:
                        scale(q + 2)
                    if trail:
                        if not last:
                            dve.wait_ge(hi_ready, f + 1)
                            dve.tensor_tensor(residue[:, 0:n, :], z, z_split[1 - i][:, 0:n, 0:H], ALU.subtract
                                              ).then_inc(res_ready, 1)
                            dve.wait_ge(mid_ready, f + 1)
                            dve.wait_ge(res_ready, f + 1)
                            dve.tensor_tensor(z_split[1 - i][:, 0:n, 2 * H:3 * H], residue[:, 0:n, :],
                                              z_split[1 - i][:, 0:n, H:2 * H], ALU.subtract).then_inc(lo_ready, 1)

                over_pairs(dve, mlp)

        @block.scalar
        def _(act):
            def records(s, h, i):
                ge(act, scattered[h], STEP * 16 * i)
                hold(act)
                act.activation(rec_now[:, h, :, 0], key_f[:, bass.ds(s * STEP, STEP)], ACT.Copy)
                act.activation(rec_now[:, h, :, 1], a_e[:, bass.ds(s * STEP, STEP)], ACT.Copy
                               ).then_inc(recs_ready, 1)

            def layernorm(t):
                rows = slice(0, LN_ROWS)
                act.wait_ge(ln_vec, 6 * t + 2)
                act.activation(ln_std[rows, :], ln_mv[rows, 1:2], ACT.Sqrt, bias=eps_col[rows, :]
                               ).then_inc(ln_act, 1)
                act.wait_ge(ln_vec, 6 * t + 4)
                ge(act, ln_out, 32 * t)
                act.activation(ln_z[rows, :], ln_y[rows, :], ACT.Relu).then_inc(ln_act, 1)
                act.activation(ln_split[rows, 0:H], ln_y[rows, :], ACT.Relu).then_inc(ln_act, 1)
                act.wait_ge(ln_vec, 6 * t + 5)
                act.activation(ln_split[rows, H:2 * H], ln_r[rows, :], ACT.Copy).then_inc(ln_act, 1)
                act.wait_ge(p_turned, t + 1)
                ge(act, p_summed, t)
                act.activation(ln_T[:, :, 0:LN_ROWS], ps[2][:, 0:H].rearrange("p (c n) -> p c n", c=HC)
                               [:, :, 0:LN_ROWS], ACT.Copy).then_inc(p_kept, 1)
                act.wait_ge(p_summed, t + 1)
                ge(act, p_stored, 16 * t)
                act.activation(ln_p[:, :, 0:LN_ROWS], ps[3][:, 0:H].rearrange("p (c n) -> p c n", c=HC)
                               [:, :, 0:LN_ROWS], ACT.Copy).then_inc(p_ready, 1)

            def four_steps(o):
                for r in range(4):
                    records(4 * o + r, r % 2, 2 * o + r // 2)
                layernorm(o)

            act.wait_ge(consts_v, 4)
            act.wait_ge(keyed, 3)
            for n in range(BUCKETS - ACT_COUNTS):
                ge(act, sided, n - 1)
                act.activation(sided_signs[n % 2], blk_b[:, :], ACT.Sign,
                               bias=under[:, ACT_COUNTS + n:ACT_COUNTS + n + 1],
                               accum_out=side[:, n:n + 1]).then_inc(sided, 1)
            act.wait_ge(keyed, 5)
            act.wait_ge(table_filled, 48)
            four_steps(0)
            with act.Fori(1, ROUNDS) as o:
                four_steps(o)
            for t in range(ROUNDS, LN_TILES):
                layernorm(t)

            act.wait_ge(table_in, 16)
            act.activation(a_all[:, :], tab[:, :, 1], ACT.Copy).then_inc(unpacked_a, 1)
            act.wait_ge(unpacked_v, 2)
            act.activation(dst_all[:, :], dst_part[:, :], ACT.Copy).then_inc(unpacked_a, 1)
            act.wait_ge(unpacked_a, 2)
            for l in range(LAYERS):
                first = l * GROUPS
                act.wait_ge(prep_v, 18 * LAYERS)
                act.wait_ge(prep_stored, 32 * LAYERS)
                if l > 0:
                    for i in range(2):
                        act.wait_ge(stored[i], 32 * fills[i] * l)

                def stage(k, g, i):
                    ge(act, landed[g], 32 * (l * PASSES + i))
                    hold(act)
                    act.activation(idx_now[:, g, :], dst_all[:, bass.ds(2 * k, 2)], ACT.Copy).then_inc(staged, 1)

                def thirds(k, g):
                    act.wait_ge(nodes_ready, 2 * (first + k + 1))
                    hold(act)
                    for j in range(2):
                        op = act.activation(hots[:, g, j, 3 * P:4 * P], hots[:, g, j, 0:P], ACT.Copy,
                                            scale=third[:, bass.ds(2 * k + j, 1)])
                    op.then_inc(thirds_ready, 1)

                def sign_rows(k, g):
                    ge(act, group_done, first + k - 3)
                    hold(act)
                    for j in range(2):
                        op = act.activation(signs[:, g, j, :], thresh[l], ACT.Sign,
                                            bias=a_all[:, bass.ds(2 * k + j, 1)], scale=-1.0)
                    op.then_inc(signs_ready, 1)

                def body(i):
                    for g in range(4):
                        stage(4 * i + g, g, i)
                        sign_rows(4 * i + g - 2, (g + 2) % 4)
                        thirds(4 * i + g - 2, (g + 2) % 4)

                for g in range(4):
                    stage(g, g, 0)
                if l == 0:
                    act.activation(parts[:, :, 0], tab[:, :, 1], ACT.Copy).then_inc(unpacked_a, 1)
                    act.wait_ge(unpacked_v, 5)
                    act.activation(parts[:, :, 1], a_rest[:, :], ACT.Copy).then_inc(unpacked_a, 1)
                for g in range(2):
                    sign_rows(g, g)
                    thirds(g, g)
                body(1)
                if l > 0:
                    with act.Fori(1, P_BODIES) as n:
                        body(2 * n)
                        act.wait_ge(p_turned, LN_TILES + n)
                        act.wait_ge(p_summed, LN_TILES + n - 1)
                        act.activation(p_T, ps[2][:, 0:H].rearrange("p (c n) -> p c n", c=HC), ACT.Copy
                                       ).then_inc(p_kept, 1)
                        body(2 * n + 1)
                        act.wait_ge(p_summed, LN_TILES + n)
                        act.wait_ge(p_stored, 16 * (LN_TILES + n - 1))
                        act.activation(p_out, ps[3][:, 0:H].rearrange("p (c n) -> p c n", c=HC), ACT.Copy
                                       ).then_inc(p_ready, 1)
                with act.Fori(2 * P_BODIES if l > 0 else 2, PASSES) as i:
                    body(i)
                for g in range(2, 4):
                    sign_rows(GROUPS - 4 + g, g)
                    thirds(GROUPS - 4 + g, g)

                mlp_first = l * PAIRS
                last = l == LAYERS - 1
                act.wait_ge(added, (l + 1) * GROUPS)

                def mlp(q, i, turn, lead, main, trail):
                    if main:
                        n = blocks_of(q)
                        act.wait_ge(pre_ready, mlp_first + q + 1)
                        for c in range(HC):
                            half = slice(c * 2 * P, c * 2 * P + n * P)
                            op = act.activation(hid[i][:, half], hid[i][:, half], ACT.Relu,
                                                bias=nb1_col[l][:, c:c + 1])
                        op.then_inc(hid_ready, 1)
                    if trail and not last:
                        f = mlp_first + q - 1
                        n = blocks_of(q - 1)
                        act.wait_ge(z_ready, f + 1)
                        ge(act, stored[1 - i], 32 * (l * fills[1 - i] + turn - 1))
                        act.activation(z_split[1 - i][:, 0:n, 0:H], z_out[1 - i][:, 0:n, :], ACT.Copy
                                       ).then_inc(hi_ready, 1)
                        act.wait_ge(res_ready, f + 1)
                        act.activation(z_split[1 - i][:, 0:n, H:2 * H], residue[:, 0:n, :], ACT.Copy
                                       ).then_inc(mid_ready, 1)
                        act.activation(pair_sums(q - 1, 0, DCOL), zero_col[:, :].rearrange("p (j n) -> p j n", j=1)
                                       .broadcast_to([P, n, DCOL]), ACT.Copy).then_inc(emptied, 1)

                over_pairs(act, mlp)

        @block.tensor
        def _(pe):
            pe.wait_ge(consts, 9)
            pe.wait_ge(counted, ACT_COUNTS + 2)
            pe.matmul(ps[0][:, 0:BUCKETS], later[:, :], counts[:, :], start=True, stop=True).then_inc(totals, 1)
            pe.matmul(ps[0][0:BUCKETS, 512:513], counts[:, :], ones[:, 0:1], start=True, stop=True
                      ).then_inc(totals, 1)
            pe.wait_ge(quot, 4)
            pe.matmul(ps[1][:, 0:BUCKETS], quot_rows[0:BUCKETS, :], later[0:BUCKETS, 0:BUCKETS],
                      start=True, stop=True).then_inc(bases, 1)
            pe.matmul(ps[1][0:BUCKETS, 512:513], later[0:BUCKETS, 0:BUCKETS], quot_f[0:BUCKETS, :],
                      start=True, stop=True).then_inc(bases, 1)
            pe.wait_ge(starts, 1)
            for n in range(2):
                op = pe.matmul(ps[n][0:1, 0:GROUPS // 2], ones[0:BLOCKS, 0:1],
                               started[0:BLOCKS, n * GROUPS // 2:(n + 1) * GROUPS // 2], start=True, stop=True)
            op.then_inc(grouped, 1)

            def times_nW1(t):
                pe.wait_ge(ln_act, 4 * t + 2)
                ge(pe, p_kept, t)
                for c in range(HC):
                    op = pe.transpose(ps[2][:, c * P:c * P + LN_ROWS], ln_z[0:LN_ROWS, c * P:(c + 1) * P],
                                      ident[0:LN_ROWS, 0:LN_ROWS])
                op.then_inc(p_turned, 1)
                pe.wait_ge(p_kept, t + 1)
                ge(pe, p_ready, t)
                for h in range(HC):
                    for c in range(HC):
                        op = pe.matmul(ps[3][:, h * P:h * P + LN_ROWS], wx_first[:, c, h * P:(h + 1) * P],
                                       ln_T[:, c, 0:LN_ROWS], start=(c == 0), stop=(c == HC - 1))
                op.then_inc(p_summed, 1)

            for l in range(LAYERS):
                pe.wait_ge(blocks_known, 2)
                pe.wait_ge(weights_in, 16 * (W_DMAS * LAYERS + 1))
                ge(pe, we_kept, l)
                for m in range(HC):
                    for c in range(HC):
                        op = pe.transpose(ps[0][:, m * H + c * P:m * H + (c + 1) * P],
                                          ew2_in[l][:, c, m * P:(m + 1) * P], ident[:, :])
                op.then_inc(ew2_turned, 1)
                pe.wait_ge(ew2_kept, l + 1)
                for c in range(HC):
                    for m in range(HC):
                        op = pe.matmul(ps[1][:, c * H:(c + 1) * H], ew2_T[l][:, m, c * P:(c + 1) * P],
                                       wa_in[l][:, m, :], start=(m == 0), stop=(m == HC - 1))
                op.then_inc(we_summed, 1)
                pe.wait_ge(we_kept, l + 1)
                pe.wait_ge(prep_v, 18 * l + 18)
                ge(pe, wd_kept, l)
                for c in range(HC):
                    pe.matmul(ps[0][0:2, 512:512 + H], d_cols[l][:, c, :], we_new[l][:, c, :], start=(c == 0),
                              stop=False)
                for c in range(HC):
                    op = pe.matmul(ps[0][0:2, 512:512 + H], d_cols[l][:, 2 + c, :], wa_in[l][:, c, :],
                                   start=False, stop=(c == HC - 1))
                op.then_inc(wd_summed, 1)
                times_nW1(l)

            with pe.Fori(LAYERS, LN_TILES) as t:
                times_nW1(t)

            for l in range(LAYERS):

                first = l * GROUPS

                def group(k, g, i):
                    pe.wait_ge(hots_ready, first + k + 1)
                    pe.wait_ge(thirds_ready, first + k + 1)
                    pe.wait_ge(signs_ready, first + k + 1)
                    ge(pe, added, first + k - (3 if l == 0 else 1))
                    acc = acc_of(l, g)
                    for j in range(2):
                        hot_j = hots[:, g, j, :]
                        for c in range(HC):
                            sg = signs[:, g, j, c * P:(c + 1) * P]
                            o = 2 * c * P
                            pe.matmul(acc[:, o:o + 2 * P], sg, hot_j[:, 0:2 * P],
                                      start=(j == 0 and c == 0), stop=False, skip_group_check=True)
                            for q in (2, 3):
                                pe.matmul(acc[:, o + P:o + 2 * P], sg, hot_j[:, q * P:(q + 1) * P],
                                          start=False, stop=(j == 1 and q == 3), skip_group_check=True)
                    pe.wait_ge(landed[g], 32 * (l * PASSES + i + 1))
                    for j in range(2):
                        hot_j = hots[:, g, j, :]
                        for c in range(HC):
                            for q in range(3):
                                op = pe.matmul(acc[:, XCOL + c * P:XCOL + (c + 1) * P],
                                               gath[:, g, j, q * H + c * P:q * H + (c + 1) * P], hot_j[:, 0:P],
                                               start=(j == 0 and c == 0 and q == 0),
                                               stop=(j == 1 and q == 2), skip_group_check=True)
                        if l == 0:
                            for q in range(4):
                                o = DCOL + min(q, 1)
                                op = pe.matmul(acc[:, o:o + 1], hot_j[:, q * P:(q + 1) * P], ones_b[:, :],
                                               start=False, stop=(j == 1 and q in (0, 3)), skip_group_check=True)
                    op.then_inc(group_done, 1)

                def body(i):
                    for g in range(4):
                        group(4 * i + g, g, i)

                body(0)
                if l > 0:
                    body(1)
                    with pe.Fori(1, P_BODIES) as n:
                        pe.wait_ge(p_here, 16 * (n + 1))
                        pe.wait_ge(p_kept, LN_TILES + n - 1)
                        for c in range(HC):
                            op = pe.transpose(ps[2][:, c * P:(c + 1) * P], p_in[:, c * P:(c + 1) * P], ident[:, :])
                        op.then_inc(p_turned, 1)
                        body(2 * n)
                        pe.wait_ge(p_kept, LN_TILES + n)
                        pe.wait_ge(p_ready, LN_TILES + n - 1)
                        for h in range(HC):
                            for c in range(HC):
                                op = pe.matmul(ps[3][:, h * P:(h + 1) * P], wx[:, c, h * P:(h + 1) * P], p_T[:, c, :],
                                               start=(c == 0), stop=(c == HC - 1))
                        op.then_inc(p_summed, 1)
                        body(2 * n + 1)
                with pe.Fori(2 * P_BODIES if l > 0 else 1, PASSES) as i:
                    body(i)

                mlp_first = l * PAIRS
                pe.wait_ge(added, (l + 1) * GROUPS)
                pe.wait_ge(weights_here, 16 * HERE_DMAS * (l + 1))

                def mlp(q, i, turn, lead, main, trail):
                    if lead:
                        f = mlp_first + q + 1
                        n = blocks_of(q + 1)
                        pe.wait_ge(d_taken, f + 1)
                        ge(pe, dT_ready, f - 1)
                        for j in range(n):
                            op = pe.transpose(ps_d[1 - i][0:2, j * P:(j + 1) * P], d_in[:, 1 - i, j, :], ident[:, :])
                        op.then_inc(turned, 1)
                    if main:
                        f = mlp_first + q
                        n = blocks_of(q)
                        pe.wait_ge(rel_ready, HC * (f + 1))
                        pe.wait_ge(dT_ready, f + 1)
                        ge(pe, hid_ready, f - 1)
                        for h in range(HC):
                            fs = slice(h * P, (h + 1) * P)
                            to = ps[i][:, (4 + 2 * h) * P:(4 + 2 * h + n) * P]
                            for c in range(HC):
                                pe.matmul(to, wa[:, c, fs], pair_sums(q, XCOL + c * P, P), start=(c == 0),
                                          stop=False)
                                pe.matmul(to, we[:, c, fs], pair_sums(q, 2 * c * P, P), start=False, stop=False)
                            op = pe.matmul(to, wd[:, fs], d_T[:, i, 0:n * P], start=False, stop=True)
                        op.then_inc(hid_summed, 1)
                    if trail:
                        f = mlp_first + q - 1
                        pe.wait_ge(hid_ready, f + 1)
                        ge(pe, z_ready, f - 1)
                        for j in range(blocks_of(q - 1)):
                            for c in range(HC):
                                o = (2 * c + j) * P
                                op = pe.matmul(ps_out[1 - i][:, j * H:(j + 1) * H], hid[1 - i][:, o:o + P], w2[:, c, :],
                                               start=(c == 0), stop=(c == HC - 1))
                        op.then_inc(out_summed, 1)

                over_pairs(pe, mlp)


_LAYER = ("eW1", "eb1", "eW2", "eb2", "nW1", "nb1", "nW2", "nb2")


def kernel(**inputs):
    import numpy as _np
    import concourse.bacc as _bacc
    from concourse import mybir as _mybir
    from concourse.bass_utils import run_bass_kernel_spmd as _run

    nc = _bacc.Bacc("TRN2", target_bir_lowering=False, num_devices=1)
    arrays = {}

    def given(name):
        a = _np.ascontiguousarray(inputs[name])
        arrays[f"in_{name}"] = a
        return nc.dram_tensor(f"in_{name}", a.shape, _mybir.dt.from_np(a.dtype), kind="ExternalInput").ap()

    edges = [given(name) for name in ("x", "src", "dst", "edge_weight1")]
    weights = [[given(f"L0_gnn_l{l}_{name}") for l in range(LAYERS)] for name in _LAYER]
    out = nc.dram_tensor("out_0", (N_NODES, H), _mybir.dt.float32, kind="ExternalOutput").ap()
    gnn(nc, *edges, *weights, out)
    r = _run(nc, [arrays], core_ids=[0])
    return r.results[0]["out_0"]
```
